# Optimizing a Trainium2 kernel written in Bass

```python
import numpy as np
import jax
import jax.numpy as jnp

def _softmax(x, axis=-1):
    return jax.nn.softmax(x, axis=axis)

def _gelu(x):
    return jax.nn.gelu(x, approximate=True)

def _silu(x):
    return jax.nn.silu(x)

def _sigmoid(x):
    return jax.nn.sigmoid(x)

def _layernorm(x, axis=-1, eps=1e-05):
    m = jnp.mean(x, axis=axis, keepdims=True)
    v = jnp.var(x, axis=axis, keepdims=True)
    return (x - m) / jnp.sqrt(v + eps)

def _scatter_add(tgt, idx, src, axis=0):
    return tgt.at[idx].add(src)

def _segment_sum(src, seg, n):
    return jax.ops.segment_sum(src, seg, n)
kernel_name = 'mk_gnn_resnorm_d2_gnn_r8_ef6e15'

def setup_inputs(seed: int=0):
    np.random.seed(seed)
    _w = jnp.asarray

    def _rec_inputs():
        import jax
        import jax.numpy as jnp
        _gk = jax.random.key(seed)
        x = -0.000202 + 1 * jax.random.normal(jax.random.fold_in(_gk, 1), (6250, 128), jnp.float32)
        _s = jax.random.randint(jax.random.fold_in(_gk, 2), (100000,), 0, 6250, jnp.int32)
        _d = jax.random.randint(jax.random.fold_in(_gk, 3), (100000,), 0, 6250, jnp.int32)
        _loop = jnp.arange(6250, dtype=jnp.int32)
        src = jnp.concatenate([_s, _d, _loop])
        dst = jnp.concatenate([_d, _s, _loop])
        _o = jnp.argsort(dst, stable=True)
        src = src[_o]
        dst = dst[_o]
        edge_type_8 = jax.random.randint(jax.random.fold_in(_gk, 13), (206250,), 0, 8, jnp.int32)
        edge_weight = jax.random.uniform(jax.random.fold_in(_gk, 14), (206250,), jnp.float32, 0.0, 0.999998)
        return (x, src, dst, edge_type_8, edge_weight)
    x, src, dst, edge_type_8, edge_weight = _rec_inputs()

    def _L0_gnn_setup():
        import jax, jax.numpy as jnp
        import numpy as np
        N_NODES = 6250
        N_EDGES = 100000
        IN_DIM = 128
        OUT_DIM = 128
        NUM_RELS = 8
        key = jax.random.key(seed)
        k_feat, k_rel, k_w, k_src, k_dst, k_rt = jax.random.split(key, 6)
        feat = jax.random.normal(k_feat, (N_NODES, IN_DIM), dtype=jnp.float32)
        limit = float(np.sqrt(6.0 / (IN_DIM + OUT_DIM)))
        rel_emb = jax.random.uniform(k_rel, (NUM_RELS, IN_DIM, OUT_DIM), dtype=jnp.float32, minval=-limit, maxval=limit)
        edge_weight = jax.random.uniform(k_w, (N_EDGES,), dtype=jnp.float32)
        src = jax.random.randint(k_src, (N_EDGES,), 0, N_NODES, dtype=jnp.int32)
        dst = jax.random.randint(k_dst, (N_EDGES,), 0, N_NODES, dtype=jnp.int32)
        rel_type = jax.random.randint(k_rt, (N_EDGES,), 0, NUM_RELS, dtype=jnp.int32)
        return {'feat': feat, 'rel_emb': rel_emb, 'edge_weight': edge_weight, 'src': src, 'dst': dst, 'rel_type': rel_type}
    _L0_gnn_all = _L0_gnn_setup()
    _L0_gnn_in = {k: v for k, v in _L0_gnn_all.items() if k in ('rel_emb',)}
    del _L0_gnn_all

    def _L1_gnn_setup():
        import jax, jax.numpy as jnp
        import numpy as np
        N_NODES = 6250
        N_EDGES = 100000
        DIM = 128
        BN_EPS = 1e-05
        key = jax.random.key(seed)
        ks = jax.random.split(key, 12)
        d = DIM
        s = 1.0 / np.sqrt(d)
        x = jax.random.normal(ks[0], (N_NODES, d), dtype=jnp.float32)
        edge_index = jax.random.randint(ks[1], (2, N_EDGES), 0, N_NODES, dtype=jnp.int64)
        W_msg = jax.random.uniform(ks[2], (d, d), jnp.float32, -s, s)
        b_msg = jax.random.uniform(ks[3], (d,), jnp.float32, -s, s)
        sa = 1.0 / np.sqrt(2 * d)
        W_att = jax.random.uniform(ks[4], (2 * d, 1), jnp.float32, -sa, sa)
        b_att = jax.random.uniform(ks[5], (1,), jnp.float32, -sa, sa)
        W_ih = jax.random.uniform(ks[6], (3 * d, d), jnp.float32, -s, s)
        b_ih = jax.random.uniform(ks[7], (3 * d,), jnp.float32, -s, s)
        W_hh = jax.random.uniform(ks[8], (3 * d, d), jnp.float32, -s, s)
        b_hh = jax.random.uniform(ks[9], (3 * d,), jnp.float32, -s, s)
        gamma = jnp.ones((d,), jnp.float32)
        beta = jnp.zeros((d,), jnp.float32)
        return {'x': x, 'edge_index': edge_index, 'W_msg': W_msg, 'b_msg': b_msg, 'W_att': W_att, 'b_att': b_att, 'W_ih': W_ih, 'b_ih': b_ih, 'W_hh': W_hh, 'b_hh': b_hh, 'gamma': gamma, 'beta': beta}
    _L1_gnn_all = _L1_gnn_setup()
    _L1_gnn_in = {k: v for k, v in _L1_gnn_all.items() if k in ('W_msg', 'b_msg', 'W_att', 'b_att', 'W_ih', 'b_ih', 'W_hh', 'b_hh', 'gamma', 'beta')}
    del _L1_gnn_all
    return {'x': x, 'src': src, 'dst': dst, 'edge_type_8': edge_type_8, 'edge_weight': edge_weight, 'L0_gnn_rel_emb': _L0_gnn_in['rel_emb'], 'L1_gnn_W_msg': _L1_gnn_in['W_msg'], 'L1_gnn_b_msg': _L1_gnn_in['b_msg'], 'L1_gnn_W_att': _L1_gnn_in['W_att'], 'L1_gnn_b_att': _L1_gnn_in['b_att'], 'L1_gnn_W_ih': _L1_gnn_in['W_ih'], 'L1_gnn_b_ih': _L1_gnn_in['b_ih'], 'L1_gnn_W_hh': _L1_gnn_in['W_hh'], 'L1_gnn_b_hh': _L1_gnn_in['b_hh'], 'L1_gnn_gamma': _L1_gnn_in['gamma'], 'L1_gnn_beta': _L1_gnn_in['beta']}

def reference(x, src, dst, edge_type_8, edge_weight, L0_gnn_rel_emb, L1_gnn_W_msg, L1_gnn_b_msg, L1_gnn_W_att, L1_gnn_b_att, L1_gnn_W_ih, L1_gnn_b_ih, L1_gnn_W_hh, L1_gnn_b_hh, L1_gnn_gamma, L1_gnn_beta):
    import jax
    import jax.numpy as jnp

    def _L0_gnn_ref(feat, rel_emb, edge_weight, src, dst, rel_type):
        import jax, jax.numpy as jnp
        import numpy as np
        N_NODES = 6250
        N_EDGES = 100000
        IN_DIM = 128
        OUT_DIM = 128
        NUM_RELS = 8
        src_feat = feat[src]
        num_rels = rel_emb.shape[0]
        msg = jnp.zeros((src_feat.shape[0], rel_emb.shape[2]), dtype=src_feat.dtype)
        for r in range(num_rels):
            mask = (rel_type == r)[:, None]
            msg = msg + jnp.where(mask, src_feat @ rel_emb[r], jnp.zeros((), dtype=src_feat.dtype))
        msg = msg * edge_weight[:, None]
        return jax.ops.segment_sum(msg, dst, num_segments=feat.shape[0])

    def _L1_gnn_ref(x, edge_index, W_msg, b_msg, W_att, b_att, W_ih, b_ih, W_hh, b_hh, gamma, beta):
        import jax, jax.numpy as jnp
        import numpy as np
        N_NODES = 6250
        N_EDGES = 100000
        DIM = 128
        BN_EPS = 1e-05
        num_nodes, d = x.shape
        src = edge_index[0]
        dst = edge_index[1]
        xs = x[src]
        xd = x[dst]
        att = jax.nn.sigmoid(xs @ W_att[:d] + xd @ W_att[d:] + b_att)
        messages = (xs @ W_msg + b_msg) * att
        aggregated = jax.ops.segment_sum(messages, dst, num_segments=num_nodes)
        gi = aggregated @ W_ih.T + b_ih
        gh = x @ W_hh.T + b_hh
        i_r, i_z, i_n = jnp.split(gi, 3, axis=1)
        h_r, h_z, h_n = jnp.split(gh, 3, axis=1)
        r = jax.nn.sigmoid(i_r + h_r)
        z = jax.nn.sigmoid(i_z + h_z)
        n = jnp.tanh(i_n + r * h_n)
        h_new = (1.0 - z) * n + z * x
        mean = jnp.mean(h_new, axis=0)
        var = jnp.var(h_new, axis=0)
        return gamma * (h_new - mean) * jax.lax.rsqrt(var + BN_EPS) + beta
    edge_index = jnp.stack([src, dst])
    x = _layernorm(x + _L0_gnn_ref(x, L0_gnn_rel_emb, edge_weight, src, dst, edge_type_8), axis=-1)
    x = _layernorm(x + _L1_gnn_ref(x, edge_index, L1_gnn_W_msg, L1_gnn_b_msg, L1_gnn_W_att, L1_gnn_b_att, L1_gnn_W_ih, L1_gnn_b_ih, L1_gnn_W_hh, L1_gnn_b_hh, L1_gnn_gamma, L1_gnn_beta), axis=-1)
    return x

_drawn_inputs = setup_inputs


def setup_inputs(seed=0):
    import zlib

    import numpy as np

    out = dict(_drawn_inputs(seed))
    spreads = {'L1_gnn_gamma': (1.0, 0.2), 'L1_gnn_beta': (0.0, 0.1)}
    factors = {'L1_gnn_b_ih': 4.217, 'L1_gnn_b_hh': 5.288}
    for name, (base, spread) in spreads.items():
        noise = np.random.default_rng([zlib.crc32(name.encode()), seed]).standard_normal(out[name].shape)
        drawn = base * np.exp(spread * noise) if base else spread * noise
        out[name] = jnp.asarray(drawn.astype(out[name].dtype))
    for name, factor in factors.items():
        out[name] = (out[name] * factor).astype(out[name].dtype)
    return out
```

```python
import concourse.bass as bass
from concourse import mybir
from contextlib import ExitStack

F32 = mybir.dt.float32
I32 = mybir.dt.int32
U32 = mybir.dt.uint32
ALU = mybir.AluOpType
ACT = mybir.ActivationFunctionType
AX = mybir.AxisListType

P = 128
NODES = 6250
FEAT = 128
RELS = 8
EDGES = 206250
EPS = 1e-5

TILES = 13
GROUP = TILES * P
GROUPS = -(-EDGES // GROUP)
LAST_EDGES = EDGES - (GROUPS - 1) * GROUP
SLOTS = 4
ROUNDS = GROUPS // SLOTS
WINDOW = 64
WINDOWS = -(-NODES // WINDOW)
BLOCKS = -(-NODES // P)
LAST_ROWS = NODES - (BLOCKS - 1) * P
PADDED = BLOCKS * P
SUM_COLS = PADDED + WINDOW
CHUNK = 448
CHUNKS = PADDED // CHUNK
MSG_ROW = FEAT + 1
NO_MATCH = -1.0
assert ROUNDS * SLOTS == GROUPS and (BLOCKS - 1) % 4 == 0 and CHUNKS * CHUNK == PADDED


def build(nc, x, src, dst, edge_type, edge_weight, rel_emb, w_msg, b_msg, w_att, b_att, w_ih, b_ih,
          w_hh, b_hh, gamma, beta, out):
    ctx = ExitStack()
    with ctx:
        def sb(name, shape, dt=F32):
            return ctx.enter_context(nc.sbuf_tensor(name, shape, dt))

        def sem(name):
            return ctx.enter_context(nc.semaphore(name))

        rel_table = nc.dram_tensor("rel_table", (NODES, RELS * FEAT), F32, kind="Internal").ap()
        rel_table_rows = rel_table.rearrange("n (r f) -> (n r) f", r=RELS)
        msg_table = nc.dram_tensor("msg_table", (NODES, MSG_ROW), F32, kind="Internal").ap()

        ident = sb("ident", [P, P])
        ones = sb("ones", [P, P])
        window_iota_i = sb("window_iota_i", [P, WINDOW], I32)
        window_iota = sb("window_iota", [P, WINDOW])
        window_start_i = sb("window_start_i", [P, WINDOWS], I32)
        window_start = sb("window_start", [P, WINDOWS])
        eps = sb("eps", [P, 1])
        rel_w = sb("rel_w", [P, RELS, FEAT])
        table_w = sb("table_w", [P, MSG_ROW])
        table_bias = sb("table_bias", [P, MSG_ROW])
        att_dst = sb("att_dst", [P, 1])
        att_dst_rep = sb("att_dst_rep", [P, P])
        w_ih_rows = sb("w_ih_rows", [P, 3, FEAT])
        w_hh_rows = sb("w_hh_rows", [P, 3, FEAT])
        w_ih_t = sb("w_ih_t", [P, 3, P])
        w_hh_t = sb("w_hh_t", [P, 3, P])
        b_ih_c = sb("b_ih_c", [P, 3])
        b_hh_c = sb("b_hh_c", [P, 3])
        gate_bias = sb("gate_bias", [P, 2])
        gamma_c = sb("gamma_c", [P, 1])
        beta_c = sb("beta_c", [P, 1])

        nodes_t = sb("nodes_t", [P, PADDED])
        sums_t = sb("sums_t", [P, SUM_COLS])
        att_rows = sb("att_rows", [P, SUM_COLS])
        node_rows = sb("node_rows", [P, PADDED])
        gathered = sb("gathered", [P, SLOTS, TILES, MSG_ROW])
        edge_words = sb("edge_words", [P, GROUPS, 4, TILES], I32)
        words = sb("words", [P, SLOTS, 4, TILES], I32)
        words_f = words[:, :, :, :].bitcast(F32)
        in_window = sb("in_window", [P, TILES])
        select = sb("select", [P, 2, TILES, WINDOW])
        x_slots = sb("x_slots", [P, 4, FEAT])
        block_slots = sb("block_slots", [P, 2, P])
        block_slots2 = sb("block_slots2", [P, 2, P])
        out_slots = sb("out_slots", [P, 4, MSG_ROW])
        stats = sb("stats", [P, BLOCKS, 6])
        norm = sb("norm", [P, 8, BLOCKS])
        bn_stats = sb("bn_stats", [P, CHUNKS, 6])
        bn = sb("bn", [P, 8])
        gru = sb("gru", [P, 2, 6, CHUNK])
        lo = sb("lo", [P, 1])
        hi = sb("hi", [P, 2])
        diag = sb("diag", [P, 2, GROUPS])
        span = sb("span", [P, 2])
        group_base = sb("group_base", [P, 1])
        base_row = sb("base_row", [P, GROUPS], I32)
        span_i = sb("span_i", [P, 1], I32)

        raw_src = att_rows[:, 0:GROUP]
        raw_type = att_rows[:, GROUP:2 * GROUP]
        raw_dst_big = att_rows[:, 2 * GROUP:3 * GROUP]
        raw_dst = node_rows[:, 0:GROUP]
        raw_weight = node_rows[:, GROUP:2 * GROUP]
        table_slots = gathered[:, :, :, :].rearrange("p s t m -> p (s t m)")[:, 0:4 * RELS * FEAT]\
            .rearrange("p (s m) -> p s m", s=4)

        psum = ctx.enter_context(nc.psum_tensor("psum", [P, 8, 512], F32))
        sigmoids = psum[:, 4:8, :].rearrange("p (s b) n -> p s (b n)", s=2)

        pads_set = sem("pads_set")
        raw_here = sem("raw_here")
        weights_here = sem("weights_here")
        ident_made = sem("ident_made")
        consts_made = sem("consts_made")
        consts_cast = sem("consts_cast")
        prep_step = sem("prep_step")
        diag_ready = sem("diag_ready")
        base_spread = sem("base_spread")
        base_ready = sem("base_ready")
        planes_ready = sem("planes_ready")
        edges_turned = sem("edges_turned")
        words_dve = sem("words_dve")
        words_act = sem("words_act")
        gates_turned = sem("gates_turned")
        gates_copied = sem("gates_copied")
        rep_ready = sem("rep_ready")
        x_here = [sem(f"x_here{s}") for s in range(4)]
        x_turned = sem("x_turned")
        xt_copied = sem("xt_copied")
        rel_mm = sem("rel_mm")
        rel_act = sem("rel_act")
        rel_dve = sem("rel_dve")
        rel_stored = [sem(f"rel_stored{s}") for s in range(4)]
        sums_clear = sem("sums_clear")
        gathers_begun = sem("gathers_begun")

        class SweepSems:
            def __init__(self, tag, slots):
                self.words_here = [sem(f"words_here_{tag}{s}") for s in range(slots)]
                self.rows_here = [sem(f"rows_here_{tag}{s}") for s in range(slots)]
                self.sigmoids_ready = sem(f"sigmoids_ready_{tag}")
                self.shifted = sem(f"shifted_{tag}")
                self.select_ready = sem(f"select_ready_{tag}")
                self.summed = sem(f"summed_{tag}")
                self.added = sem(f"added_{tag}")

        one_window = [SweepSems(f"one{layer}_", SLOTS) for layer in range(2)]
        all_windows = [SweepSems(f"all{layer}_", 1) for layer in range(2)]
        sweep_done = [sem(f"sweep_done{layer}") for layer in range(2)]
        xa_here = [sem(f"xa_here{s}") for s in range(4)]
        sum_block = sem("sum_block")
        sum_turned = sem("sum_turned")
        rows_added = sem("rows_added")
        stats_ready = [sem(f"stats_ready{n}") for n in range(2)]
        norm_step = [sem(f"norm_step{n}") for n in range(2)]
        std_ready = [sem(f"std_ready{n}") for n in range(2)]
        x1_block = sem("x1_block")
        x1_turned = sem("x1_turned")
        x1_copied = sem("x1_copied")
        x1_slot = sem("x1_slot")
        msg_mm = sem("msg_mm")
        msg_biased = sem("msg_biased")
        msg_stored = [sem(f"msg_stored{s}") for s in range(4)]
        att_mm = sem("att_mm")
        att_copied = sem("att_copied")
        att_end_clear = sem("att_end_clear")
        gates_mm = sem("gates_mm")
        rz_ready = sem("rz_ready")
        n_input = sem("n_input")
        n_step = sem("n_step")
        n_ready = sem("n_ready")
        h_step = sem("h_step")
        h_ready = sem("h_ready")
        h_stats = sem("h_stats")
        bn_step = sem("bn_step")
        bn_std = sem("bn_std")
        bn_ready = sem("bn_ready")
        y_scaled = sem("y_scaled")
        y_block = sem("y_block")
        y_turned = sem("y_turned")
        y_copied = sem("y_copied")
        y_stats = sem("y_stats")
        out_ready = sem("out_ready")
        out_stored = [sem(f"out_stored{s}") for s in range(4)]

        block = ctx.enter_context(nc.Block())

        def over_blocks(engine, body):
            with engine.Fori(0, (BLOCKS - 1) // 4) as r:
                for s in range(4):
                    body(r * 4 + s, r, s)
            body(BLOCKS - 1, (BLOCKS - 1) // 4, 0)

        def columns(i, width):
            return slice(i * width, (i + 1) * width) if isinstance(i, int) else bass.ds(i * width, width)

        def fits(engine, one, every):
            span_value = engine.value_load(span_i[0:1, 0:1], min_val=0, max_val=NODES)
            with engine.If(span_value < WINDOW):
                one()
            with engine.Else():
                every()

        @block.sync
        def _(sp):
            sp.wait_ge(pads_set, 5)
            for to, array, dt in ((raw_dst_big, dst, I32), (raw_dst, dst, I32), (raw_src, src, I32),
                                  (raw_type, edge_type, I32), (raw_weight, edge_weight, F32)):
                full = (GROUPS - 1) * GROUP
                to = to if dt == F32 else to.bitcast(dt)
                sp.dma_start(to[0:GROUPS - 1, :],
                             array[0:full].rearrange("(g e) -> g e", e=GROUP)).then_inc(raw_here, 16)
                sp.dma_start(to[GROUPS - 1:GROUPS, 0:LAST_EDGES],
                             array[full:EDGES].rearrange("(g e) -> g e", g=1)).then_inc(raw_here, 16)

            def load_x(i, r, s):
                sp.wait_ge(x_turned, i + 1)
                rows = LAST_ROWS if isinstance(i, int) and i == BLOCKS - 1 else P
                sp.dma_start(x_slots[0:rows, s, :], x[bass.ds(i * P, rows), :]).then_inc(x_here[s], 16)
            over_blocks(sp, load_x)

            def words_one(layer):
                sems = one_window[layer]

                def run():
                    with sp.Fori(0, ROUNDS) as r:
                        for s in range(SLOTS):
                            g = r * SLOTS + s
                            sp.wait_ge(sems.added, g + 1)
                            sp.dma_start(words[:, s, :, :].rearrange("p w t -> p (w t)"),
                                         edge_words[:, :, :, :].rearrange("p g w t -> p (g w t)")[
                                             :, bass.ds(g * 4 * TILES, 4 * TILES)])\
                              .then_inc(sems.words_here[s], 16)
                return run

            def words_all(layer):
                sems = all_windows[layer]

                def run():
                    with sp.Fori(0, GROUPS) as g:
                        sp.wait_ge(sems.added, g * WINDOWS + 1)
                        sp.dma_start(words[:, 0, :, :].rearrange("p w t -> p (w t)"),
                                     edge_words[:, :, :, :].rearrange("p g w t -> p (g w t)")[
                                         :, bass.ds(g * 4 * TILES, 4 * TILES)])\
                          .then_inc(sems.words_here[0], 16)
                return run

            sp.wait_ge(words_dve, TILES)
            sp.wait_ge(words_act, TILES)
            fits(sp, words_one(0), words_all(0))

            def load_xa(i, r, s):
                sp.wait_ge(rows_added, i + 1)
                rows = LAST_ROWS if isinstance(i, int) and i == BLOCKS - 1 else P
                sp.dma_start(x_slots[0:rows, s, :], x[bass.ds(i * P, rows), :]).then_inc(xa_here[s], 16)
            over_blocks(sp, load_xa)

            def store_messages(i, r, s):
                sp.wait_ge(msg_biased, i + 5)
                rows = LAST_ROWS if isinstance(i, int) and i == BLOCKS - 1 else P
                sp.dma_start(msg_table[bass.ds(i * P, rows), :], out_slots[0:rows, s, :])\
                  .then_inc(msg_stored[s], 16)
            over_blocks(sp, store_messages)

            fits(sp, words_one(1), words_all(1))

            def store_out(i, r, s):
                sp.wait_ge(out_ready, i + 1)
                rows = LAST_ROWS if isinstance(i, int) and i == BLOCKS - 1 else P
                sp.dma_start(out[bass.ds(i * P, rows), :], out_slots[0:rows, s, 0:FEAT])\
                  .then_inc(out_stored[s], 16)
            over_blocks(sp, store_out)
            for s in range(4):
                sp.wait_ge(out_stored[s], 16 * ((BLOCKS - 1) // 4 + (2 if s == 0 else 1)))

        @block.gpsimd
        def _(pool):
            pool.memset(ident[:, :], 0.0).then_inc(ident_made, 1)
            pool.memset(ones[:, :], 1.0).then_inc(consts_made, 1)
            pool.memset(eps[:, :], EPS).then_inc(consts_made, 1)
            pool.iota(window_iota_i[:, :], pattern=[[1, WINDOW]], base=0, channel_multiplier=0)\
                .then_inc(consts_made, 1)
            pool.iota(window_start_i[:, :], pattern=[[WINDOW, WINDOWS]], base=0, channel_multiplier=0)\
                .then_inc(consts_made, 1)
            pool.wait_ge(ident_made, 1)
            pool.affine_select(out=ident[:, :], in_=ident[:, :], compare_op=ALU.not_equal, fill=1.0,
                               base=0, pattern=[[-1, P]], channel_multiplier=1).then_inc(ident_made, 1)
            pool.memset(sums_t[:, :], 0.0).then_inc(sums_clear, 1)

            def gather_group(table, width, plane, s, rows_here):
                pool.sem_inc(gathers_begun, 1)
                for t in range(TILES):
                    pool.indirect_dma_start(
                        out=gathered[:, s, t, 0:width], out_offset=None, in_=table,
                        in_offset=bass.IndirectOffsetOnAxis(ap=words[:, s, plane, t:t + 1].bitcast(U32),
                                                            axis=0)).then_inc(rows_here, 16)

            def gather_one(layer, table, width):
                sems = one_window[layer]

                def run():
                    with pool.Fori(0, ROUNDS) as r:
                        for s in range(SLOTS):
                            pool.wait_ge(sems.words_here[s], (r + 1) * 16)
                            gather_group(table, width, 2 + layer, s, sems.rows_here[s])
                return run

            def gather_all(layer, table, width):
                sems = all_windows[layer]

                def run():
                    with pool.Fori(0, GROUPS) as g:
                        pool.wait_ge(sems.words_here[0], (g + 1) * 16)
                        gather_group(table, width, 2 + layer, 0, sems.rows_here[0])
                return run

            for s in range(4):
                pool.wait_ge(rel_stored[s], 16 * ((BLOCKS - 1) // 4 + (2 if s == 0 else 1)))
            pool.wait_ge(base_ready, 1)
            fits(pool, gather_one(0, rel_table_rows, FEAT), gather_all(0, rel_table_rows, FEAT))

            pool.wait_ge(rows_added, BLOCKS + 4)
            pool.memset(sums_t[:, :], 0.0).then_inc(sums_clear, 1)
            for s in range(4):
                pool.wait_ge(msg_stored[s], 16 * ((BLOCKS - 1) // 4 + (2 if s == 0 else 1)))
            fits(pool, gather_one(1, msg_table, MSG_ROW), gather_all(1, msg_table, MSG_ROW))

        @block.scalar
        def _(act):
            act.sem_inc(rel_act, 2)
            act.sem_inc(x1_copied, 2)
            for s in range(4):
                act.sem_inc(rel_stored[s], 16)
                act.sem_inc(msg_stored[s], 16)
                act.sem_inc(out_stored[s], 16)
            act.dma_start(rel_w[:, :, :], rel_emb.rearrange("r f o -> f r o")).then_inc(weights_here, 16)
            act.dma_start(table_w[:, 0:FEAT], w_msg).then_inc(weights_here, 16)
            act.dma_start(table_w[:, FEAT:MSG_ROW], w_att[0:FEAT, :]).then_inc(weights_here, 16)
            act.dma_start(att_dst[:, :], w_att[FEAT:2 * FEAT, :]).then_inc(weights_here, 16)
            act.dma_start(table_bias[:, 0:FEAT],
                          b_msg.rearrange("(a f) -> a f", a=1).broadcast_to((P, b_msg.shape[0]))).then_inc(weights_here, 16)
            act.dma_start(table_bias[:, FEAT:MSG_ROW],
                          b_att.rearrange("(a f) -> a f", a=1).broadcast_to((P, 1))).then_inc(weights_here, 16)
            act.dma_start(w_ih_rows[:, :, :], w_ih.rearrange("(g p) f -> p g f", p=P)).then_inc(weights_here, 16)
            act.dma_start(w_hh_rows[:, :, :], w_hh.rearrange("(g p) f -> p g f", p=P)).then_inc(weights_here, 16)
            act.dma_start(b_ih_c[:, :], b_ih.rearrange("(g p) -> p g", p=P), allow_slow_non_contiguous=True).then_inc(weights_here, 16)
            act.dma_start(b_hh_c[:, :], b_hh.rearrange("(g p) -> p g", p=P), allow_slow_non_contiguous=True).then_inc(weights_here, 16)
            act.dma_start(gamma_c[:, :], gamma.rearrange("(p a) -> p a", a=1)).then_inc(weights_here, 16)
            act.dma_start(beta_c[:, :], beta.rearrange("(p a) -> p a", a=1)).then_inc(weights_here, 16)

            for t in range(TILES):
                act.wait_ge(edges_turned, t + 1)
                nc.scalar.activation(
                    edge_words[:, :, 2:4, t].rearrange("p g w -> p w g"),
                    psum[:, 2 + t % 2, 0:256].rearrange("p (w g) -> p w g", w=2)[:, :, 0:GROUPS],
                    ACT.Copy).then_inc(words_act, 1)

            def evacuate(i, r, s):
                act.wait_ge(rel_mm, i + 3)
                act.wait_ge(rel_stored[s], (r + 1) * 16)
                nc.scalar.activation(table_slots[:, s, 0:512], psum[:, 4 + 2 * (s % 2), :], ACT.Copy)\
                  .then_inc(rel_act, 1)
                act.wait_ge(rel_act, i + 3)
                act.wait_ge(rel_dve, i + 3)
                rows = LAST_ROWS if isinstance(i, int) and i == BLOCKS - 1 else P
                act.dma_start(rel_table[bass.ds(i * P, rows), :], table_slots[0:rows, s, :])\
                   .then_inc(rel_stored[s], 16)
            over_blocks(act, evacuate)

            act.wait_ge(sweep_done[0], 1)

            def copy_sums(i, r, s):
                act.wait_ge(sum_turned, i + 1)
                nc.scalar.activation(block_slots[:, s % 2, :], sums_t[:, columns(i, P)], ACT.Copy)\
                  .then_inc(sum_block, 1)
            over_blocks(act, copy_sums)

            act.wait_ge(norm_step[0], 5)
            nc.scalar.activation(norm[:, 5, :], norm[:, 4, :], ACT.Sqrt, bias=eps[:, 0:1])\
              .then_inc(std_ready[0], 1)

            def copy_x1(i, r, s):
                act.wait_ge(x1_turned, i + 3)
                nc.scalar.activation(nodes_t[:, columns(i, P)], psum[:, s % 2, 0:P], ACT.Copy)\
                  .then_inc(x1_copied, 1)
            over_blocks(act, copy_x1)

            def x1_to_slot(i, r, s):
                act.wait_ge(x1_copied, i + 3)
                act.wait_ge(msg_mm, i + 1)
                nc.scalar.activation(block_slots2[:, s % 2, :], nodes_t[:, columns(i, P)], ACT.Copy)\
                  .then_inc(x1_slot, 1)
            over_blocks(act, x1_to_slot)

            with act.Fori(0, CHUNKS) as j:
                act.wait_ge(att_mm, j + 1)
                nc.scalar.activation(att_rows[:, bass.ds(j * CHUNK, CHUNK)], psum[:, 4, 0:CHUNK], ACT.Copy)\
                  .then_inc(att_copied, 1)
            act.wait_ge(att_copied, CHUNKS + 1)
            act.wait_ge(att_end_clear, 1)

            def sigmoid_tiles(source, s, half, sems):
                for t in range(TILES):
                    last = nc.scalar.activation(sigmoids[:, half, t * WINDOW:(t + 1) * WINDOW], source,
                                                ACT.Sigmoid, bias=gathered[:, s, t, FEAT:MSG_ROW])
                last.then_inc(sems.sigmoids_ready, 1)

            def sigmoids_one():
                sems = one_window[1]
                with act.Fori(0, ROUNDS) as r:
                    for s in range(SLOTS):
                        g = r * SLOTS + s
                        base = act.value_load(base_row[0:1, bass.ds(g, 1)], min_val=0, max_val=NODES - 1)
                        act.wait_ge(sems.rows_here[s], (r + 1) * (16 * TILES))
                        act.wait_ge(sems.select_ready, g + 1)
                        sigmoid_tiles(att_rows[:, bass.ds(base, WINDOW)], s, s % 2, sems)

            def sigmoids_all():
                sems = all_windows[1]
                with act.Fori(0, GROUPS) as g:
                    with act.Fori(0, WINDOWS) as w:
                        act.wait_ge(sems.rows_here[0], (g + 1) * (16 * TILES))
                        act.wait_ge(sems.added, g * WINDOWS + w + 1)
                        sigmoid_tiles(att_rows[:, bass.ds(w * WINDOW, WINDOW)], 0, 0, sems)
            fits(act, sigmoids_one, sigmoids_all)

            def gates(j, half):
                act.wait_ge(gates_mm, j + 1)
                for gate in range(2):
                    nc.scalar.activation(gru[:, half, gate, :], psum[:, 4 * half + gate, 0:CHUNK],
                                         ACT.Sigmoid, bias=gate_bias[:, gate:gate + 1]).then_inc(rz_ready, 1)
                act.wait_ge(n_input, j + 1)
                nc.scalar.activation(gru[:, half, 3, :], gru[:, half, 2, :], ACT.Tanh, bias=b_ih_c[:, 2:3])\
                  .then_inc(n_ready, 1)
            with act.Fori(0, CHUNKS // 2) as r:
                for half in range(2):
                    gates(r * 2 + half, half)

            act.wait_ge(bn_step, 1)
            nc.scalar.activation(bn[:, 2:3], bn[:, 1:2], ACT.Sqrt, bias=eps[:, 0:1]).then_inc(bn_std, 1)

            act.wait_ge(bn_ready, 1)

            def scale_h(i, r, s):
                act.wait_ge(y_block, i + 1)
                nc.scalar.activation(block_slots[:, s % 2, :], sums_t[:, columns(i, P)], ACT.Identity,
                                     bias=bn[:, 6:7], scale=bn[:, 4:5]).then_inc(y_scaled, 1)
                act.wait_ge(y_turned, i + 3)
                nc.scalar.activation(node_rows[:, columns(i, P)], psum[:, s % 2, 0:P], ACT.Copy)\
                  .then_inc(y_copied, 1)
            over_blocks(act, scale_h)

            act.wait_ge(norm_step[1], 5)
            nc.scalar.activation(norm[:, 5, :], norm[:, 4, :], ACT.Sqrt, bias=eps[:, 0:1])\
              .then_inc(std_ready[1], 1)

        @block.tensor
        def _(pe):
            pe.sem_inc(rel_mm, 2)
            pe.sem_inc(x_turned, 4)
            pe.sem_inc(sum_turned, 2)
            pe.sem_inc(x1_turned, 2)
            pe.sem_inc(msg_mm, 2)
            pe.sem_inc(y_turned, 2)
            for layer in range(2):
                pe.sem_inc(one_window[layer].summed, 2)

            pe.wait_ge(ident_made, 2)
            pe.wait_ge(consts_made, 4)
            pe.wait_ge(diag_ready, 2)
            for n in range(2):
                last = nc.tensor.matmul(psum[:, 7, n * GROUPS:(n + 1) * GROUPS], ones[0:GROUPS, :],
                                        diag[0:GROUPS, n, :], start=True, stop=True)
            last.then_inc(base_spread, 1)

            pe.wait_ge(weights_here, 12 * 16)
            for gate in range(3):
                nc.tensor.transpose(psum[:, 5, gate * P:(gate + 1) * P], w_ih_rows[:, gate, :], ident[:, :])
                last = nc.tensor.transpose(psum[:, 6, gate * P:(gate + 1) * P], w_hh_rows[:, gate, :],
                                           ident[:, :])
            last.then_inc(gates_turned, 1)

            pe.wait_ge(planes_ready, 1)
            planes = (raw_dst, raw_weight, raw_type, raw_src)
            for t in range(TILES):
                if t >= 2:
                    pe.wait_ge(words_act, t - 1)
                    pe.wait_ge(words_dve, t - 1)
                for w, plane in enumerate(planes):
                    last = nc.tensor.transpose(psum[:, t % 2 + 2 * (w // 2), (w % 2) * P:(w % 2) * P + GROUPS],
                                               plane[0:GROUPS, t * P:(t + 1) * P],
                                               ident[0:GROUPS, 0:GROUPS])
                last.then_inc(edges_turned, 1)

            def turn_x(i, r, s):
                pe.wait_ge(x_here[s], (r + 1) * 16)
                pe.wait_ge(xt_copied, i + 1)
                nc.tensor.transpose(psum[:, 2 + s % 2, 0:P], x_slots[:, s, :], ident[:, :])\
                  .then_inc(x_turned, 1)

            def multiply_x(i, r, s):
                pe.wait_ge(xt_copied, i + 3)
                pe.wait_ge(rel_act, i + 1)
                pe.wait_ge(rel_dve, i + 1)
                for half in range(2):
                    last = nc.tensor.matmul(psum[:, 4 + 2 * (s % 2) + half, :], block_slots[:, s % 2, :],
                                            rel_w[:, 4 * half:4 * half + 4, :].rearrange("p r o -> p (r o)"),
                                            start=True, stop=True)
                last.then_inc(rel_mm, 1)
            pe.wait_ge(words_act, TILES)
            pe.wait_ge(words_dve, TILES)
            pe.wait_ge(gates_copied, 1)
            pe.wait_ge(base_ready, 1)
            turn_x(0, 0, 0)

            def both(i, r, s):
                turn_x(i + 1, r + (s + 1) // 4, (s + 1) % 4)
                multiply_x(i, r, s)
            with pe.Fori(0, (BLOCKS - 1) // 4) as r:
                for s in range(4):
                    both(r * 4 + s, r, s)
            multiply_x(BLOCKS - 1, (BLOCKS - 1) // 4, 0)

            def sum_group(width, s, half, bank, sems):
                for t in range(TILES):
                    last = nc.tensor.matmul(psum[:, bank, 0:WINDOW], gathered[:, s, t, 0:FEAT],
                                            select[:, half, t, :], start=(t == 0), stop=(t == TILES - 1))
                last.then_inc(sems.summed, 1)

            def sum_one(layer):
                sems = one_window[layer]

                def run():
                    with pe.Fori(0, ROUNDS) as r:
                        for s in range(SLOTS):
                            g = r * SLOTS + s
                            pe.wait_ge(sems.rows_here[s], (r + 1) * (16 * TILES))
                            pe.wait_ge(sems.added, g + 1)
                            pe.wait_ge(sems.select_ready, g + 3)
                            sum_group(FEAT, s, s % 2, s, sems)
                return run

            def sum_all(layer):
                sems = all_windows[layer]

                def run():
                    with pe.Fori(0, GROUPS) as g:
                        with pe.Fori(0, WINDOWS) as w:
                            pe.wait_ge(sems.rows_here[0], (g + 1) * (16 * TILES))
                            pe.wait_ge(sems.select_ready, g * WINDOWS + w + 1)
                            sum_group(FEAT, 0, 0, 0, sems)
                return run
            fits(pe, sum_one(0), sum_all(0))

            def turn_sums(i, r, s):
                pe.wait_ge(sum_block, i + 1)
                pe.wait_ge(rows_added, i + 3)
                nc.tensor.transpose(psum[:, s % 2, 0:P], block_slots[:, s % 2, :], ident[:, :])\
                  .then_inc(sum_turned, 1)
            over_blocks(pe, turn_sums)

            def turn_x1(i, r, s):
                pe.wait_ge(x1_block, i + 1)
                pe.wait_ge(x1_copied, i + 1)
                nc.tensor.transpose(psum[:, s % 2, 0:P], block_slots[:, s % 2, :], ident[:, :])\
                  .then_inc(x1_turned, 1)
            over_blocks(pe, turn_x1)

            def multiply_x1(i, r, s):
                pe.wait_ge(x1_slot, i + 1)
                pe.wait_ge(msg_biased, i + 3)
                nc.tensor.matmul(psum[:, 2 + s % 2, 0:MSG_ROW], block_slots2[:, s % 2, :], table_w[:, :],
                                 start=True, stop=True).then_inc(msg_mm, 1)
            over_blocks(pe, multiply_x1)

            pe.wait_ge(rep_ready, 1)
            with pe.Fori(0, CHUNKS) as j:
                pe.wait_ge(att_copied, j + 1)
                nc.tensor.matmul(psum[:, 4, 0:CHUNK], att_dst_rep[:, :], nodes_t[:, bass.ds(j * CHUNK, CHUNK)],
                                 start=True, stop=True).then_inc(att_mm, 1)

            fits(pe, sum_one(1), sum_all(1))

            pe.wait_ge(sweep_done[1], 1)

            def gate_products(j, half):
                pe.wait_ge(h_ready, j + 1)
                cols = bass.ds(j * CHUNK, CHUNK)
                for gate in range(2):
                    nc.tensor.matmul(psum[:, 4 * half + gate, 0:CHUNK], w_ih_t[:, gate, :], sums_t[:, cols],
                                     start=True, stop=False)
                    nc.tensor.matmul(psum[:, 4 * half + gate, 0:CHUNK], w_hh_t[:, gate, :], nodes_t[:, cols],
                                     start=False, stop=True)
                nc.tensor.matmul(psum[:, 4 * half + 2, 0:CHUNK], w_ih_t[:, 2, :], sums_t[:, cols],
                                 start=True, stop=True)
                nc.tensor.matmul(psum[:, 4 * half + 3, 0:CHUNK], w_hh_t[:, 2, :], nodes_t[:, cols],
                                 start=True, stop=True).then_inc(gates_mm, 1)
            with pe.Fori(0, CHUNKS // 2) as r:
                for half in range(2):
                    gate_products(r * 2 + half, half)

            def turn_y(i, r, s):
                pe.wait_ge(y_block, i + 3)
                pe.wait_ge(y_copied, i + 1)
                nc.tensor.transpose(psum[:, s % 2, 0:P], block_slots2[:, s % 2, :], ident[:, :])\
                  .then_inc(y_turned, 1)
            over_blocks(pe, turn_y)

        @block.vector
        def _(dve):
            v = nc.vector
            dve.sem_inc(xt_copied, 2)
            dve.sem_inc(rel_dve, 2)
            dve.sem_inc(rows_added, 4)
            dve.sem_inc(msg_biased, 4)
            dve.sem_inc(att_copied, 1)
            dve.sem_inc(h_ready, 2)
            dve.sem_inc(y_block, 2)
            dve.sem_inc(y_copied, 2)
            for layer in range(2):
                dve.sem_inc(one_window[layer].added, SLOTS)
                dve.sem_inc(one_window[layer].select_ready, 2)
                dve.sem_inc(all_windows[layer].added, 1)

            tail = slice(LAST_EDGES, GROUP)
            v.memset(raw_dst_big.bitcast(I32)[96:P, tail], 1 << 20).then_inc(pads_set, 1)
            v.memset(raw_dst.bitcast(I32)[96:P, tail], int(NO_MATCH)).then_inc(pads_set, 1)
            v.memset(raw_src[96:P, tail], 0.0).then_inc(pads_set, 1)
            v.memset(raw_type[96:P, tail], 0.0).then_inc(pads_set, 1)
            v.memset(raw_weight[96:P, tail], 0.0).then_inc(pads_set, 1)
            dve.wait_ge(consts_made, 4)
            v.tensor_copy(window_iota[:, :], window_iota_i[:, :]).then_inc(consts_cast, 1)
            v.tensor_copy(window_start[:, :], window_start_i[:, :]).then_inc(consts_cast, 1)

            g = slice(0, GROUPS)
            steps = [0]

            def step(instruction):
                steps[0] += 1
                instruction.then_inc(prep_step, 1)
                dve.wait_ge(prep_step, steps[0])
            dve.wait_ge(raw_here, 10 * 16)
            v.tensor_reduce(lo[g, :], raw_dst_big.bitcast(I32)[g, :], AX.X, ALU.min).then_inc(prep_step, 1)
            step(v.tensor_reduce(hi[g, 0:1], raw_dst.bitcast(I32)[g, :], AX.X, ALU.max))
            steps[0] += 1
            dve.wait_ge(prep_step, steps[0])
            step(v.tensor_sub(hi[g, 1:2], hi[g, 0:1], lo[g, :]))
            dve.wait_ge(ident_made, 2)
            v.tensor_scalar(diag[g, 0, :], ident[g, g], lo[g, :], None, ALU.mult).then_inc(diag_ready, 1)
            v.tensor_scalar(diag[g, 1, :], ident[g, g], hi[g, 1:2], None, ALU.mult).then_inc(diag_ready, 1)
            v.tensor_copy(raw_src[g, :], raw_src.bitcast(I32)[g, :]).then_inc(prep_step, 1)
            v.tensor_copy(raw_dst[g, :], raw_dst.bitcast(I32)[g, :]).then_inc(prep_step, 1)
            steps[0] += 2
            dve.wait_ge(prep_step, steps[0])
            v.scalar_tensor_tensor(raw_type[g, :], raw_src[g, :], float(RELS), raw_type.bitcast(I32)[g, :],
                                   ALU.mult, ALU.add).then_inc(prep_step, 1)
            steps[0] += 1
            dve.wait_ge(base_spread, 1)
            step(v.tensor_reduce(span[:, 0:1], psum[:, 7, GROUPS:2 * GROUPS], AX.X, ALU.max))
            step(v.tensor_scalar(span[:, 1:2], span[:, 0:1], float(WINDOW), None, ALU.is_lt))
            step(v.tensor_mul(group_base[g, :], lo[g, :], span[g, 1:2]))
            step(v.tensor_copy(span_i[:, :], span[:, 0:1]))
            step(v.tensor_scalar(base_row[:, :], psum[:, 7, 0:GROUPS], span[:, 1:2], None, ALU.mult))
            v.tensor_scalar(raw_dst[g, :], raw_dst[g, :], group_base[g, :], None, ALU.subtract)\
             .then_inc(planes_ready, 1)
            dve.drain().then_inc(base_ready, 1)

            dve.wait_ge(gates_turned, 1)
            v.tensor_copy(w_ih_t[:, :, :].rearrange("p g o -> p (g o)"), psum[:, 5, 0:3 * P])
            v.tensor_copy(w_hh_t[:, :, :].rearrange("p g o -> p (g o)"), psum[:, 6, 0:3 * P])
            v.tensor_add(gate_bias[:, :], b_ih_c[:, 0:2], b_hh_c[:, 0:2])
            v.tensor_scalar(att_dst_rep[:, :], ones[:, :], att_dst[:, 0:1], None, ALU.mult)\
             .then_inc(rep_ready, 1)
            dve.drain().then_inc(gates_copied, 1)

            for t in range(TILES):
                dve.wait_ge(edges_turned, t + 1)
                v.tensor_copy(edge_words[:, :, 0:2, t].rearrange("p g w -> p w g").bitcast(F32),
                              psum[:, t % 2, 0:256].rearrange("p (w g) -> p w g", w=2)[:, :, 0:GROUPS])\
                 .then_inc(words_dve, 1)

            def copy_xt(i, r, s):
                dve.wait_ge(x_turned, i + 5)
                dve.wait_ge(rel_mm, i + 1)
                v.tensor_copy(block_slots[:, s % 2, :], psum[:, 2 + s % 2, 0:P]).then_inc(xt_copied, 1)

            def evacuate(i, r, s):
                dve.wait_ge(rel_mm, i + 3)
                dve.wait_ge(rel_stored[s], (r + 1) * 16)
                v.tensor_copy(table_slots[:, s, 512:1024], psum[:, 5 + 2 * (s % 2), :]).then_inc(rel_dve, 1)
            copy_xt(0, 0, 0)
            with dve.Fori(0, (BLOCKS - 1) // 4) as r:
                for s in range(4):
                    copy_xt(r * 4 + s + 1, r + (s + 1) // 4, (s + 1) % 4)
                    evacuate(r * 4 + s, r, s)
            evacuate(BLOCKS - 1, (BLOCKS - 1) // 4, 0)

            def select_tiles(layer, s, half, places, sems):
                for t in range(TILES):
                    if layer == 0:
                        last = v.tensor_scalar(select[:, half, t, :], window_iota[:, :], places[:, t:t + 1],
                                               words_f[:, s, 1, t:t + 1], ALU.is_equal, ALU.mult)
                    else:
                        last = v.scalar_tensor_tensor(
                            select[:, half, t, :], window_iota[:, :], places[:, t:t + 1],
                            sigmoids[:, half, t * WINDOW:(t + 1) * WINDOW], ALU.is_equal, ALU.mult)
                last.then_inc(sems.select_ready, 1)

            def sweep_one(layer):
                sems = one_window[layer]

                def run():
                    with dve.Fori(0, ROUNDS) as r:
                        for s in range(SLOTS):
                            g = r * SLOTS + s
                            dve.wait_ge(sems.words_here[s], (r + 1) * 16)
                            dve.wait_ge(sems.summed, g + 1)
                            if layer == 1:
                                dve.wait_ge(sems.sigmoids_ready, g + 1)
                            select_tiles(layer, s, s % 2, words_f[:, s, 0, :], sems)
                            base = dve.value_load(base_row[0:1, bass.ds(g, 1)], min_val=0,
                                                  max_val=NODES - 1)
                            dve.wait_ge(sems.summed, g + 3)
                            dve.wait_ge(sems.added, g + SLOTS)
                            to = sums_t[:, bass.ds(base, WINDOW)]
                            v.tensor_add(to, to, psum[:, s, 0:WINDOW]).then_inc(sems.added, 1)
                return run

            def sweep_all(layer):
                sems = all_windows[layer]

                def run():
                    with dve.Fori(0, GROUPS) as g:
                        with dve.Fori(0, WINDOWS) as w:
                            dve.wait_ge(sems.words_here[0], (g + 1) * 16)
                            done = g * WINDOWS + w
                            dve.wait_ge(sems.added, done + 1)
                            v.tensor_scalar(in_window[:, :], words_f[:, 0, 0, :],
                                            window_start[:, bass.ds(w, 1)], None, ALU.subtract)\
                             .then_inc(sems.shifted, 1)
                            dve.wait_ge(sems.shifted, done + 1)
                            if layer == 1:
                                dve.wait_ge(sems.sigmoids_ready, done + 1)
                            select_tiles(layer, 0, 0, in_window, sems)
                            dve.wait_ge(sems.summed, done + 1)
                            to = sums_t[:, bass.ds(w * WINDOW, WINDOW)]
                            v.tensor_add(to, to, psum[:, 0, 0:WINDOW]).then_inc(sems.added, 1)
                return run

            dve.wait_ge(consts_cast, 2)
            dve.wait_ge(sums_clear, 1)
            fits(dve, sweep_one(0), sweep_all(0))
            dve.drain().then_inc(sweep_done[0], 1)

            def add_rows(i, r, s):
                dve.wait_ge(xa_here[s], (r + 1) * 16)
                dve.wait_ge(sum_turned, i + 3)
                v.tensor_add(node_rows[:, columns(i, P)], x_slots[:, s, :], psum[:, s % 2, 0:P])\
                 .then_inc(rows_added, 1)
                dve.wait_ge(rows_added, i + 5)
                v.bn_stats(stats[:, columns(i, 1), :].rearrange("p i s -> p (i s)"),
                           node_rows[:, columns(i, P)]).then_inc(stats_ready[0], 1)
            over_blocks(dve, add_rows)

            def normalisers(n):
                sems = norm_step[n]
                dve.wait_ge(stats_ready[n], BLOCKS)
                v.tensor_add(norm[:, 1, :], stats[:, :, 1], stats[:, :, 4]).then_inc(sems, 1)
                v.tensor_sub(norm[:, 2, :], stats[:, :, 1], stats[:, :, 4]).then_inc(sems, 1)
                v.tensor_add(norm[:, 3, :], stats[:, :, 2], stats[:, :, 5]).then_inc(sems, 1)
                dve.wait_ge(sems, 3)
                v.tensor_scalar(norm[:, 0, :], norm[:, 1, :], 0.5, None, ALU.mult)
                v.tensor_scalar(norm[:, 3, :], norm[:, 3, :], 1.0 / FEAT, None, ALU.mult)
                v.scalar_tensor_tensor(norm[:, 7, :], norm[:, 2, :], 0.25, norm[:, 2, :], ALU.mult, ALU.mult)\
                 .then_inc(sems, 1)
                dve.wait_ge(sems, 4)
                v.tensor_add(norm[:, 4, :], norm[:, 7, :], norm[:, 3, :]).then_inc(sems, 1)
                dve.wait_ge(std_ready[n], 1)
                v.reciprocal(norm[:, 6, :], norm[:, 5, :]).then_inc(sems, 1)
                dve.wait_ge(sems, 6)
            normalisers(0)

            def x1_rows(i, r, s):
                dve.wait_ge(x1_turned, i + 1)
                v.tensor_scalar(block_slots[:, s % 2, :], node_rows[:, columns(i, P)],
                                norm[:, 0, columns(i, 1)], norm[:, 6, columns(i, 1)],
                                ALU.subtract, ALU.mult).then_inc(x1_block, 1)
            over_blocks(dve, x1_rows)

            def bias_messages(i, r, s):
                dve.wait_ge(msg_mm, i + 3)
                dve.wait_ge(msg_stored[s], (r + 1) * 16)
                v.tensor_add(out_slots[:, s, :], psum[:, 2 + s % 2, 0:MSG_ROW], table_bias[:, :])\
                 .then_inc(msg_biased, 1)
            over_blocks(dve, bias_messages)
            v.memset(att_rows[:, PADDED:SUM_COLS], 0.0).then_inc(att_end_clear, 1)

            dve.wait_ge(sums_clear, 2)
            fits(dve, sweep_one(1), sweep_all(1))
            dve.drain().then_inc(sweep_done[1], 1)

            def update(j, half, valid):
                cols = bass.ds(j * CHUNK, CHUNK)
                slot = gru[:, half, :, :]
                dve.wait_ge(rz_ready, j * 2 + 2)
                v.scalar_tensor_tensor(slot[:, 4, :], psum[:, 4 * half + 3, 0:CHUNK], b_hh_c[:, 2:3],
                                       slot[:, 0, :], ALU.add, ALU.mult).then_inc(n_step, 1)
                dve.wait_ge(n_step, j + 1)
                v.tensor_add(slot[:, 2, :], slot[:, 4, :], psum[:, 4 * half + 2, 0:CHUNK]).then_inc(n_input, 1)
                dve.wait_ge(n_ready, j + 1)
                v.tensor_sub(slot[:, 5, :], nodes_t[:, cols], slot[:, 3, :]).then_inc(h_step, 1)
                dve.wait_ge(h_step, j * 2 + 1)
                v.tensor_mul(slot[:, 5, :], slot[:, 5, :], slot[:, 1, :]).then_inc(h_step, 1)
                dve.wait_ge(h_step, j * 2 + 2)
                v.tensor_add(sums_t[:, cols], slot[:, 5, :], slot[:, 3, :]).then_inc(h_ready, 1)
                dve.wait_ge(h_ready, j + 3)
                v.bn_stats(bn_stats[:, columns(j, 1), :].rearrange("p i s -> p (i s)"),
                           sums_t[:, bass.ds(j * CHUNK, valid)]).then_inc(h_stats, 1)
            with dve.Fori(0, CHUNKS // 2 - 1) as r:
                for half in range(2):
                    update(r * 2 + half, half, CHUNK)
            update(CHUNKS - 2, 0, CHUNK)
            update(CHUNKS - 1, 1, NODES - (CHUNKS - 1) * CHUNK)

            dve.wait_ge(h_stats, CHUNKS)
            v.bn_aggr(bn[:, 0:2], bn_stats[:, :, :].rearrange("p j s -> p (j s)")).then_inc(bn_step, 1)
            dve.wait_ge(bn_std, 1)
            v.reciprocal(bn[:, 3:4], bn[:, 2:3]).then_inc(bn_step, 1)
            dve.wait_ge(bn_step, 2)
            v.tensor_mul(bn[:, 4:5], bn[:, 3:4], gamma_c[:, :]).then_inc(bn_step, 1)
            dve.wait_ge(bn_step, 3)
            v.tensor_mul(bn[:, 5:6], bn[:, 0:1], bn[:, 4:5]).then_inc(bn_step, 1)
            dve.wait_ge(bn_step, 4)
            v.tensor_sub(bn[:, 6:7], beta_c[:, :], bn[:, 5:6]).then_inc(bn_ready, 1)

            def add_y(i, r, s):
                dve.wait_ge(y_scaled, i + 1)
                dve.wait_ge(y_turned, i + 1)
                v.tensor_add(block_slots2[:, s % 2, :], block_slots[:, s % 2, :], nodes_t[:, columns(i, P)])\
                 .then_inc(y_block, 1)
                dve.wait_ge(y_copied, i + 3)
                v.bn_stats(stats[:, columns(i, 1), :].rearrange("p i s -> p (i s)"), node_rows[:, columns(i, P)])\
                 .then_inc(y_stats, 1)
            over_blocks(dve, add_y)
            dve.wait_ge(y_stats, BLOCKS)
            dve.drain().then_inc(stats_ready[1], BLOCKS)
            dve.wait_ge(y_copied, BLOCKS + 2)
            normalisers(1)

            def out_rows(i, r, s):
                dve.wait_ge(out_stored[s], (r + 1) * 16)
                v.tensor_scalar(out_slots[:, s, 0:FEAT], node_rows[:, columns(i, P)],
                                norm[:, 0, columns(i, 1)], norm[:, 6, columns(i, 1)],
                                ALU.subtract, ALU.mult).then_inc(out_ready, 1)
            over_blocks(dve, out_rows)


INPUTS = ["x", "src", "dst", "edge_type_8", "edge_weight", "L0_gnn_rel_emb", "L1_gnn_W_msg",
          "L1_gnn_b_msg", "L1_gnn_W_att", "L1_gnn_b_att", "L1_gnn_W_ih", "L1_gnn_b_ih",
          "L1_gnn_W_hh", "L1_gnn_b_hh", "L1_gnn_gamma", "L1_gnn_beta"]


def kernel(**inputs):
    import numpy as np
    import concourse.bacc as bacc
    from concourse import mybir as mb
    from concourse.bass_utils import run_bass_kernel_spmd

    nc = bacc.Bacc("TRN2", target_bir_lowering=False, num_devices=1)
    arrays, args = {}, []
    for name in INPUTS:
        a = np.ascontiguousarray(inputs[name])
        arrays[f"in_{name}"] = a
        args.append(nc.dram_tensor(f"in_{name}", a.shape, mb.dt.from_np(a.dtype), kind="ExternalInput").ap())
    out = nc.dram_tensor("out", (NODES, FEAT), F32, kind="ExternalOutput").ap()
    build(nc, *args, out)
    result = run_bass_kernel_spmd(nc, [arrays], core_ids=[0])
    return result.results[0]["out"]
```

```python
import concourse.bass as bass
from concourse import mybir
from contextlib import ExitStack

F32 = mybir.dt.float32
I32 = mybir.dt.int32
F16 = mybir.dt.float16
U32 = mybir.dt.uint32
ALU = mybir.AluOpType
ACT = mybir.ActivationFunctionType
AX = mybir.AxisListType

P = 128
NODES = 6250
FEAT = 128
RELS = 8
EDGES = 206250
EPS = 1e-5

TILES = 13
GROUP = TILES * P
GROUPS = -(-EDGES // GROUP)
LAST_EDGES = EDGES - (GROUPS - 1) * GROUP
SLOTS = 4
ROUNDS = GROUPS // SLOTS
WINDOW = 58
WINDOWS = -(-NODES // WINDOW)
BLOCKS = -(-NODES // P)
LAST_ROWS = NODES - (BLOCKS - 1) * P
PADDED = BLOCKS * P
SUM_COLS = PADDED + WINDOW
CHUNK = 448
CHUNKS = PADDED // CHUNK
MSG_ROW = FEAT + 1
MSG_ALL = FEAT + 2
PANEL = 8
PANELS = -(-GROUPS // PANEL)
LAST_PANEL = GROUPS - (PANELS - 1) * PANEL
CHUNK_BLOCKS = 7
COUNT_CHUNKS = BLOCKS // CHUNK_BLOCKS
BANK_BLOCKS = 8
BANKS = -(-BLOCKS // BANK_BLOCKS)
BANK_COLS = BANK_BLOCKS * WINDOW
PANEL_COLS = PANEL * WINDOW
TILE_WINDOW = 16
KEYS = BLOCKS * TILE_WINDOW
TILE_START = [min(max(round(P * NODES / EDGES * t) - 5, 0), WINDOW - TILE_WINDOW) for t in range(TILES)]
HOT_SLOTS = 4
WORDS = 6
ROWS_WORD = 4
COUNT_COLS = BLOCKS * WINDOW
NO_MATCH = -1.0
assert TILE_START[-1] + TILE_WINDOW == WINDOW and PANELS % 2 == 0 and COUNT_CHUNKS * CHUNK_BLOCKS == BLOCKS
assert ROUNDS * SLOTS == GROUPS and (BLOCKS - 1) % 4 == 0 and CHUNKS * CHUNK == PADDED


def build(nc, x, src, dst, edge_type, edge_weight, rel_emb, w_msg, b_msg, w_att, b_att, w_ih, b_ih,
          w_hh, b_hh, gamma, beta, out):
    ctx = ExitStack()
    with ctx:
        def sb(name, shape, dt=F32):
            return ctx.enter_context(nc.sbuf_tensor(name, shape, dt))

        def sem(name):
            return ctx.enter_context(nc.semaphore(name))

        rel_table = nc.dram_tensor("rel_table", (NODES, RELS * FEAT), F32, kind="Internal").ap()
        rel_table_rows = rel_table.rearrange("n (r f) -> (n r) f", r=RELS)
        count_table = nc.dram_tensor("count_table", (GROUPS, P, COUNT_COLS), F16, kind="Internal").ap()
        edge_table = nc.dram_tensor("edge_table", (P, GROUPS * WORDS * TILES), I32, kind="Internal").ap()
        msg_table = nc.dram_tensor("msg_table", (NODES, MSG_ROW), F32, kind="Internal").ap()

        ident = sb("ident", [P, P])
        ones = sb("ones", [P, P])
        window_iota_i = sb("window_iota_i", [P, WINDOW], I32)
        window_iota = sb("window_iota", [P, WINDOW])
        window_start_i = sb("window_start_i", [P, WINDOWS], I32)
        window_start = sb("window_start", [P, WINDOWS])
        eps = sb("eps", [P, 1])
        rel_w = sb("rel_w", [P, RELS, FEAT])
        table_w = sb("table_w", [P, MSG_ALL])
        table_bias = sb("table_bias", [P, MSG_ALL])
        att_dst = sb("att_dst", [P, 1])
        att_dst_rep = sb("att_dst_rep", [P, P])
        w_ih_t = sb("w_ih_t", [P, 3, P])
        w_hh_t = sb("w_hh_t", [P, 3, P])
        b_ih_c = sb("b_ih_c", [P, 3])
        b_hh_c = sb("b_hh_c", [P, 3])
        gate_bias = sb("gate_bias", [P, 2])
        gamma_c = sb("gamma_c", [P, 1])
        beta_c = sb("beta_c", [P, 1])

        node_space = sb("node_space", [P, PADDED + SUM_COLS])
        nodes_t = node_space[:, 0:PADDED]
        sums_t = node_space[:, PADDED:]
        att_rows = sb("att_rows", [P, SUM_COLS])
        row_space = sb("row_space", [P, BLOCKS * MSG_ALL])
        node_rows = row_space[:, 0:PADDED]
        msg_rows = row_space[:, :].rearrange("p (b m) -> p b m", b=BLOCKS)
        stage_space = sb("stage_space", [P, COUNT_CHUNKS * CHUNK_BLOCKS * PANEL_COLS // 2])
        gather_space = stage_space[:, 0:SLOTS * TILES * MSG_ROW]
        gathered = gather_space.rearrange("p (s t m) -> p s t m", s=SLOTS, t=TILES)
        counts_out_slots = stage_space[:, SLOTS * TILES * MSG_ROW:SLOTS * TILES * MSG_ROW + COUNT_COLS]\
            .bitcast(F16).rearrange("p (s n) -> p s n", s=2)
        counts = stage_space[:, :].bitcast(F16).rearrange("p (c g n) -> p c g n", c=COUNT_CHUNKS, g=PANEL)
        words = sb("words", [P, SLOTS, WORDS, TILES], I32)
        words_f = words[:, :, :, :].bitcast(F32)
        edge_words = node_space[:, 0:GROUPS * WORDS * TILES].bitcast(I32)\
            .rearrange("p (g w t) -> p g w t", g=GROUPS, w=WORDS)
        factors = sb("factors", [P, CHUNK_BLOCKS, PANEL_COLS])
        hot_space = factors[:, :, :].rearrange("p c n -> p (c n)").bitcast(F16)
        key_hot = hot_space[:, 0:HOT_SLOTS * KEYS].rearrange("p (s n) -> p s n", s=HOT_SLOTS)
        lo_hot = hot_space[:, HOT_SLOTS * KEYS:HOT_SLOTS * (KEYS + P)].rearrange("p (s n) -> p s n", s=HOT_SLOTS)
        key_iota = hot_space[:, HOT_SLOTS * (KEYS + P):HOT_SLOTS * (KEYS + P) + KEYS]
        q_panel = sb("q_panel", [P, 2, PANEL_COLS])
        tile_starts = sb("tile_starts", [P, TILES])
        in_window = sb("in_window", [P, TILES])
        select = sb("select", [P, 2, TILES, WINDOW])
        x_slots = sb("x_slots", [P, 4, FEAT])
        block_slots = sb("block_slots", [P, 2, P])
        block_slots2 = sb("block_slots2", [P, 2, P])
        out_slots = sb("out_slots", [P, 4, MSG_ROW])
        stats = sb("stats", [P, BLOCKS, 6])
        norm = sb("norm", [P, 8, BLOCKS])
        bn_stats = sb("bn_stats", [P, CHUNKS, 6])
        bn = sb("bn", [P, 8])
        lo = sb("lo", [P, TILES + 1])
        hi = sb("hi", [P, TILES])
        low_miss = sb("low_miss", [P, TILES])
        miss = sb("miss", [P, TILES + 1])
        diag = sb("diag", [P, 2, GROUPS])
        case = sb("case", [P, 2])
        group_base = sb("group_base", [P, 1])
        base_row = sb("base_row", [P, PANEL + GROUPS], I32)
        case_i = sb("case_i", [P, 1], I32)

        raw_src = att_rows[:, 0:GROUP]
        raw_type = att_rows[:, GROUP:2 * GROUP]
        raw_dst_big = att_rows[:, 2 * GROUP:3 * GROUP]
        raw_key = raw_dst_big
        raw_dst = row_space[:, 0:GROUP]
        raw_weight = row_space[:, GROUP:2 * GROUP]
        raw_lo = row_space[:, 2 * GROUP:3 * GROUP]
        w_rows = gather_space[:, 4 * RELS * FEAT:4 * RELS * FEAT + 6 * FEAT].rearrange("p (w g f) -> p w g f", w=2, g=3)
        w_ih_rows = w_rows[:, 0, :, :]
        w_hh_rows = w_rows[:, 1, :, :]
        gru = gather_space[:, 0:12 * CHUNK].rearrange("p (s n c) -> p s n c", s=2, n=6)
        key_iota_i = gather_space[:, 5 * RELS * FEAT:5 * RELS * FEAT + KEYS].bitcast(I32)
        assert 5 * RELS * FEAT + KEYS <= SLOTS * TILES * MSG_ROW
        table_slots = gather_space[:, 0:4 * RELS * FEAT]\
            .rearrange("p (s m) -> p s m", s=4)

        psum = ctx.enter_context(nc.psum_tensor("psum", [P, 8, 512], F32))

        pads_set = sem("pads_set")
        raw_here = sem("raw_here")
        weights_here = sem("weights_here")
        ident_made = sem("ident_made")
        consts_made = sem("consts_made")
        consts_cast = sem("consts_cast")
        prep_step = sem("prep_step")
        diag_ready = sem("diag_ready")
        base_spread = sem("base_spread")
        base_ready = sem("base_ready")
        starts_made = sem("starts_made")
        base_clear = sem("base_clear")
        key_iota_made = sem("key_iota_made")
        bias_clear = sem("bias_clear")
        planes_ready = sem("planes_ready")
        edges_turned = sem("edges_turned")
        words_dve = sem("words_dve")
        words_act = sem("words_act")
        words_stored = sem("words_stored")
        gates_turned = sem("gates_turned")
        gates_copied = sem("gates_copied")
        rep_ready = sem("rep_ready")
        x_here = [sem(f"x_here{s}") for s in range(4)]
        x_turned = sem("x_turned")
        xt_copied = sem("xt_copied")
        rel_mm = sem("rel_mm")
        rel_act = sem("rel_act")
        rel_dve = sem("rel_dve")
        rel_stored = [sem(f"rel_stored{s}") for s in range(4)]
        sums_clear = sem("sums_clear")
        gathers_begun = sem("gathers_begun")

        class GatherSems:
            def __init__(self, tag, slots):
                self.words_here = [sem(f"words_here_{tag}{s}") for s in range(slots)]
                self.rows_here = [sem(f"rows_here_{tag}{s}") for s in range(slots)]
                self.sigmoids_ready = sem(f"sigmoids_ready_{tag}")
                self.shifted = sem(f"shifted_{tag}")
                self.select_ready = sem(f"select_ready_{tag}")
                self.summed = sem(f"summed_{tag}")
                self.added = sem(f"added_{tag}")

        one_window = GatherSems("one", SLOTS)
        all_windows = [GatherSems(f"all{layer}_", 1) for layer in range(2)]
        hot_ready = sem("hot_ready")
        hot_used = sem("hot_used")
        counts_out = sem("counts_out")
        counts_stored = [sem(f"counts_stored{s}") for s in range(2)]
        counts_here = [sem(f"counts_here{c}") for c in range(COUNT_CHUNKS)]
        q_ready = sem("q_ready")
        sigmoids_ready = sem("sigmoids_ready")
        factors_ready = sem("factors_ready")
        factors_used = sem("factors_used")
        panel_added = sem("panel_added")
        sweep_done = [sem(f"sweep_done{layer}") for layer in range(2)]
        xa_here = [sem(f"xa_here{s}") for s in range(4)]
        sum_block = sem("sum_block")
        sum_turned = sem("sum_turned")
        rows_added = sem("rows_added")
        stats_ready = [sem(f"stats_ready{n}") for n in range(2)]
        norm_step = [sem(f"norm_step{n}") for n in range(2)]
        std_ready = [sem(f"std_ready{n}") for n in range(2)]
        x1_block = sem("x1_block")
        x1_turned = sem("x1_turned")
        x1_copied = sem("x1_copied")
        x1_slot = sem("x1_slot")
        msg_mm = sem("msg_mm")
        msg_biased = sem("msg_biased")
        msg_stored = [sem(f"msg_stored{s}") for s in range(4)]
        att_mm = sem("att_mm")
        att_copied = sem("att_copied")
        att_end_clear = sem("att_end_clear")
        gates_mm = sem("gates_mm")
        rz_ready = sem("rz_ready")
        n_input = sem("n_input")
        n_step = sem("n_step")
        n_ready = sem("n_ready")
        h_step = sem("h_step")
        h_ready = sem("h_ready")
        h_stats = sem("h_stats")
        bn_step = sem("bn_step")
        bn_std = sem("bn_std")
        bn_ready = sem("bn_ready")
        y_scaled = sem("y_scaled")
        y_block = sem("y_block")
        y_turned = sem("y_turned")
        y_copied = sem("y_copied")
        y_stats = sem("y_stats")
        out_ready = sem("out_ready")
        out_stored = [sem(f"out_stored{s}") for s in range(4)]

        block = ctx.enter_context(nc.Block())

        def bank_width(c):
            return min(BANK_BLOCKS, BLOCKS - c * BANK_BLOCKS) * WINDOW

        def over_blocks(engine, body):
            with engine.Fori(0, (BLOCKS - 1) // 4) as r:
                for s in range(4):
                    body(r * 4 + s, r, s)
            body(BLOCKS - 1, (BLOCKS - 1) // 4, 0)

        def msg_block(i):
            return row_space[:, columns(i, MSG_ALL)]

        def columns(i, width):
            return slice(i * width, (i + 1) * width) if isinstance(i, int) else bass.ds(i * width, width)

        def by_case(engine, windows_fit, every):
            case_value = engine.value_load(case_i[0:1, 0:1], min_val=0, max_val=1)
            with engine.If(case_value < 1):
                windows_fit()
            with engine.Else():
                every()

        def over_panels(engine, body):
            with engine.Fori(0, PANELS // 2 - 1) as turn:
                for parity in range(2):
                    body(turn * 2 + parity, turn, parity, PANEL)
            body(PANELS - 2, PANELS // 2 - 1, 0, PANEL)
            body(PANELS - 1, PANELS // 2 - 1, 1, LAST_PANEL)

        WORD_COLS = WORDS * TILES

        def load_words(sp, g, s, here):
            sp.dma_start(words[:, s, :, :].rearrange("p w t -> p (w t)"),
                         edge_table[:, columns(g, WORD_COLS)]).then_inc(here, 16)

        @block.sync
        def _(sp):
            sp.wait_ge(pads_set, 5)
            for to, array, dt in ((raw_dst_big, dst, I32), (raw_dst, dst, I32), (raw_src, src, I32),
                                  (raw_type, edge_type, I32), (raw_weight, edge_weight, F32)):
                full = (GROUPS - 1) * GROUP
                to = to if dt == F32 else to.bitcast(dt)
                sp.dma_start(to[0:GROUPS - 1, :],
                             array[0:full].rearrange("(g e) -> g e", e=GROUP)).then_inc(raw_here, 16)
                sp.dma_start(to[GROUPS - 1:GROUPS, 0:LAST_EDGES],
                             array[full:EDGES].rearrange("(g e) -> g e", g=1)).then_inc(raw_here, 16)

            def load_x(i, r, s):
                sp.wait_ge(x_turned, i + 1)
                rows = LAST_ROWS if isinstance(i, int) and i == BLOCKS - 1 else P
                sp.dma_start(x_slots[0:rows, s, :], x[bass.ds(i * P, rows), :]).then_inc(x_here[s], 16)

            sp.wait_ge(words_dve, TILES)
            sp.wait_ge(words_act, TILES)
            sp.dma_start(edge_table, edge_words.rearrange("p g w t -> p (g w t)")).then_inc(words_stored, 16)
            over_blocks(sp, load_x)
            sp.wait_ge(words_stored, 16)

            def words_layer0():
                with sp.Fori(0, ROUNDS) as r:
                    for s in range(SLOTS):
                        g = r * SLOTS + s
                        sp.wait_ge(one_window.added, g + 1)
                        load_words(sp, g, s, one_window.words_here[s])

            def words_all(layer):
                sems = all_windows[layer]

                def run():
                    with sp.Fori(0, GROUPS) as g:
                        sp.wait_ge(sems.added, g * WINDOWS + 1)
                        load_words(sp, g, 0, sems.words_here[0])
                return run

            by_case(sp, words_layer0, words_all(0))

            def load_xa(i, r, s):
                sp.wait_ge(rows_added, i + 1)
                rows = LAST_ROWS if isinstance(i, int) and i == BLOCKS - 1 else P
                sp.dma_start(x_slots[0:rows, s, :], x[bass.ds(i * P, rows), :]).then_inc(xa_here[s], 16)
            over_blocks(sp, load_xa)

            def counts_layer1():
                for s in range(2):
                    sp.wait_ge(counts_stored[s], 16 * (2 * ROUNDS + 1))

                def load_counts(k, turn, parity, groups):
                    for c in range(COUNT_CHUNKS):
                        sp.wait_ge(factors_ready, k * BLOCKS + (c + 1) * CHUNK_BLOCKS)
                        cols = slice(c * CHUNK_BLOCKS * WINDOW, (c + 1) * CHUNK_BLOCKS * WINDOW)
                        counts_from = count_table[bass.ds(k * PANEL, groups), :, cols]
                        sp.dma_start(counts[:, c, 0:groups, :], counts_from.rearrange("g p n -> p g n"))\
                          .then_inc(counts_here[c], 16)
                over_panels(sp, load_counts)

            def tables_layer1():
                sp.wait_ge(msg_biased, BLOCKS + 4)

                def store_messages(i, r, s):
                    rows = LAST_ROWS if isinstance(i, int) and i == BLOCKS - 1 else P
                    sp.dma_start(msg_table[bass.ds(i * P, rows), :], msg_block(i)[0:rows, 0:MSG_ROW])\
                      .then_inc(msg_stored[s], 16)
                over_blocks(sp, store_messages)
                words_all(1)()
            by_case(sp, counts_layer1, tables_layer1)

            def store_out(i, r, s):
                sp.wait_ge(out_ready, i + 1)
                rows = LAST_ROWS if isinstance(i, int) and i == BLOCKS - 1 else P
                sp.dma_start(out[bass.ds(i * P, rows), :], out_slots[0:rows, s, 0:FEAT])\
                  .then_inc(out_stored[s], 16)
            over_blocks(sp, store_out)
            for s in range(4):
                sp.wait_ge(out_stored[s], 16 * ((BLOCKS - 1) // 4 + (2 if s == 0 else 1)))

        @block.gpsimd
        def _(pool):
            pool.memset(ident[:, :], 0.0).then_inc(ident_made, 1)
            pool.memset(ones[:, :], 1.0).then_inc(consts_made, 1)
            pool.memset(eps[:, :], EPS).then_inc(consts_made, 1)
            pool.iota(window_iota_i[:, :], pattern=[[1, WINDOW]], base=0, channel_multiplier=0)\
                .then_inc(consts_made, 1)
            pool.iota(key_iota_i, pattern=[[1, KEYS]], base=0, channel_multiplier=0)\
                .then_inc(key_iota_made, 1)
            pool.iota(window_start_i[:, :], pattern=[[WINDOW, WINDOWS]], base=0, channel_multiplier=0)\
                .then_inc(consts_made, 1)
            pool.wait_ge(ident_made, 1)
            pool.affine_select(out=ident[:, :], in_=ident[:, :], compare_op=ALU.not_equal, fill=1.0,
                               base=0, pattern=[[-1, P]], channel_multiplier=1).then_inc(ident_made, 1)
            for t in range(TILES):
                last = pool.memset(tile_starts[:, t:t + 1], float(TILE_START[t]))
            last.then_inc(starts_made, 1)
            pool.memset(base_row[:, :], 0).then_inc(base_clear, 1)
            pool.wait_ge(words_stored, 16)
            pool.memset(sums_t[:, :], 0.0).then_inc(sums_clear, 1)

            def gather_group(table, width, plane, s, rows_here):
                pool.sem_inc(gathers_begun, 1)
                for t in range(TILES):
                    pool.indirect_dma_start(
                        out=gathered[:, s, t, 0:width], out_offset=None, in_=table,
                        in_offset=bass.IndirectOffsetOnAxis(ap=words[:, s, plane, t:t + 1].bitcast(U32),
                                                            axis=0)).then_inc(rows_here, 16)

            def gather_layer0():
                sems = one_window
                with pool.Fori(0, ROUNDS) as r:
                    for s in range(SLOTS):
                        pool.wait_ge(sems.words_here[s], (r + 1) * 16)
                        gather_group(rel_table_rows, FEAT, ROWS_WORD, s, sems.rows_here[s])

            def gather_all(layer, table, width):
                sems = all_windows[layer]

                def run():
                    with pool.Fori(0, GROUPS) as g:
                        pool.wait_ge(sems.words_here[0], (g + 1) * 16)
                        gather_group(table, width, ROWS_WORD + layer, 0, sems.rows_here[0])
                return run

            for s in range(4):
                pool.wait_ge(rel_stored[s], 16 * ((BLOCKS - 1) // 4 + (2 if s == 0 else 1)))
            pool.wait_ge(base_ready, 1)
            pool.wait_ge(consts_cast, 3)
            by_case(pool, gather_layer0, gather_all(0, rel_table_rows, FEAT))

            pool.wait_ge(rows_added, BLOCKS + 4)
            pool.memset(sums_t[:, :], 0.0).then_inc(sums_clear, 1)

            def q_windows():
                def fill(k, turn, parity, groups):
                    pool.wait_ge(sigmoids_ready, (k + 1) * BLOCKS)
                    for i in range(groups):
                        base = pool.value_load(base_row[0:1, bass.ds(k * PANEL + PANEL + i, 1)], min_val=0,
                                               max_val=NODES - 1)
                        last = pool.tensor_copy(q_panel[:, parity, i * WINDOW:(i + 1) * WINDOW],
                                                att_rows[:, bass.ds(base, WINDOW)])
                    last.then_inc(q_ready, 1)
                pool.wait_ge(att_copied, CHUNKS + 1)
                pool.wait_ge(att_end_clear, 1)
                over_panels(pool, fill)

            def gather_messages():
                for s in range(4):
                    pool.wait_ge(msg_stored[s], 16 * ((BLOCKS - 1) // 4 + (2 if s == 0 else 1)))
                gather_all(1, msg_table, MSG_ROW)()
            by_case(pool, q_windows, gather_messages)

        @block.scalar
        def _(act):
            act.sem_inc(rel_act, 2)
            act.sem_inc(x1_copied, 2)
            act.sem_inc(counts_out, 1)
            act.sem_inc(sigmoids_ready, 2 * BLOCKS)
            for s in range(2):
                act.sem_inc(counts_stored[s], 16)
            for s in range(4):
                act.sem_inc(rel_stored[s], 16)
                act.sem_inc(msg_stored[s], 16)
                act.sem_inc(out_stored[s], 16)
            act.dma_start(rel_w[:, :, :], rel_emb.rearrange("r f o -> f r o")).then_inc(weights_here, 16)
            act.dma_start(table_w[:, 0:FEAT], w_msg).then_inc(weights_here, 16)
            act.dma_start(table_w[:, FEAT:MSG_ROW], w_att[0:FEAT, :]).then_inc(weights_here, 16)
            act.dma_start(table_w[:, MSG_ROW:MSG_ALL], w_att[FEAT:2 * FEAT, :]).then_inc(weights_here, 16)
            act.dma_start(att_dst[:, :], w_att[FEAT:2 * FEAT, :]).then_inc(weights_here, 16)
            act.dma_start(table_bias[:, 0:FEAT],
                          b_msg.rearrange("(a f) -> a f", a=1).broadcast_to((P, b_msg.shape[0]))).then_inc(weights_here, 16)
            act.dma_start(table_bias[:, FEAT:MSG_ROW],
                          b_att.rearrange("(a f) -> a f", a=1).broadcast_to((P, 1))).then_inc(weights_here, 16)
            act.dma_start(w_ih_rows[:, :, :], w_ih.rearrange("(g p) f -> p g f", p=P)).then_inc(weights_here, 16)
            act.dma_start(w_hh_rows[:, :, :], w_hh.rearrange("(g p) f -> p g f", p=P)).then_inc(weights_here, 16)
            act.dma_start(b_ih_c[:, :], b_ih.rearrange("(g p) -> p g", p=P), allow_slow_non_contiguous=True).then_inc(weights_here, 16)
            act.dma_start(b_hh_c[:, :], b_hh.rearrange("(g p) -> p g", p=P), allow_slow_non_contiguous=True).then_inc(weights_here, 16)
            act.dma_start(gamma_c[:, :], gamma.rearrange("(p a) -> p a", a=1)).then_inc(weights_here, 16)
            act.dma_start(beta_c[:, :], beta.rearrange("(p a) -> p a", a=1)).then_inc(weights_here, 16)

            for t in range(TILES):
                act.wait_ge(edges_turned, t + 1)
                nc.scalar.activation(
                    edge_words[:, :, ROWS_WORD:WORDS, t].rearrange("p g w -> p w g"),
                    psum[:, 2 + t % 2, 0:256].rearrange("p (w g) -> p w g", w=2)[:, :, 0:GROUPS],
                    ACT.Copy).then_inc(words_act, 1)

            def evacuate(i, r, s):
                act.wait_ge(rel_mm, i + 3)
                act.wait_ge(rel_stored[s], (r + 1) * 16)
                nc.scalar.activation(table_slots[:, s, 0:512], psum[:, 4 + 2 * (s % 2), :], ACT.Copy)\
                  .then_inc(rel_act, 1)
                act.wait_ge(rel_act, i + 3)
                act.wait_ge(rel_dve, i + 3)
                rows = LAST_ROWS if isinstance(i, int) and i == BLOCKS - 1 else P
                act.dma_start(rel_table[bass.ds(i * P, rows), :], table_slots[0:rows, s, :])\
                   .then_inc(rel_stored[s], 16)
            over_blocks(act, evacuate)

            def counts_layer0():
                with act.Fori(0, ROUNDS) as r:
                    for s in range(SLOTS):
                        g = r * SLOTS + s
                        act.wait_ge(hot_used, g * TILES + TILES + HOT_SLOTS)
                        act.wait_ge(counts_stored[s % 2], (r * 2 + s // 2 + 1) * 16)
                        for c in range(BANKS):
                            last = nc.scalar.activation(
                                counts_out_slots[:, s % 2, c * BANK_COLS:c * BANK_COLS + bank_width(c)],
                                psum[:, 1 + c, 0:bank_width(c)], ACT.Copy)
                        last.then_inc(counts_out, 1)
                        act.wait_ge(counts_out, g + 2)
                        act.dma_start(count_table[bass.ds(g, 1), :, :].rearrange("a p n -> (a p) n"),
                                      counts_out_slots[:, s % 2, :]).then_inc(counts_stored[s % 2], 16)

            def nothing():
                act.nop()
            act.wait_ge(base_ready, 1)
            by_case(act, counts_layer0, nothing)

            act.wait_ge(sweep_done[0], 1)

            def copy_sums(i, r, s):
                act.wait_ge(sum_turned, i + 1)
                nc.scalar.activation(block_slots[:, s % 2, :], sums_t[:, columns(i, P)], ACT.Copy)\
                  .then_inc(sum_block, 1)
            over_blocks(act, copy_sums)

            act.wait_ge(norm_step[0], 5)
            nc.scalar.activation(norm[:, 5, :], norm[:, 4, :], ACT.Sqrt, bias=eps[:, 0:1])\
              .then_inc(std_ready[0], 1)

            def copy_x1(i, r, s):
                act.wait_ge(x1_turned, i + 3)
                nc.scalar.activation(nodes_t[:, columns(i, P)], psum[:, s % 2, 0:P], ACT.Copy)\
                  .then_inc(x1_copied, 1)
            over_blocks(act, copy_x1)

            def x1_to_slot(i, r, s):
                act.wait_ge(x1_copied, i + 3)
                act.wait_ge(msg_mm, i + 1)
                nc.scalar.activation(block_slots2[:, s % 2, :], nodes_t[:, columns(i, P)], ACT.Copy)\
                  .then_inc(x1_slot, 1)
            over_blocks(act, x1_to_slot)

            with act.Fori(0, CHUNKS) as j:
                act.wait_ge(att_mm, j + 1)
                nc.scalar.activation(att_rows[:, bass.ds(j * CHUNK, CHUNK)], psum[:, 4, 0:CHUNK], ACT.Copy)\
                  .then_inc(att_copied, 1)
            act.wait_ge(att_copied, CHUNKS + 1)
            act.wait_ge(att_end_clear, 1)

            def sigmoids_layer1():
                act.wait_ge(msg_biased, BLOCKS + 4)

                def squash(k, turn, parity, groups):
                    act.wait_ge(q_ready, k + 1)
                    for b in range(BLOCKS):
                        act.wait_ge(factors_used, k * BLOCKS + b + 1)
                        nc.scalar.activation(factors[:, b % CHUNK_BLOCKS, 0:groups * WINDOW],
                                             q_panel[:, parity, 0:groups * WINDOW], ACT.Sigmoid,
                                             bias=msg_rows[:, b, FEAT:MSG_ROW]).then_inc(sigmoids_ready, 1)
                over_panels(act, squash)

            def sigmoids_all():
                sems = all_windows[1]
                with act.Fori(0, GROUPS) as g:
                    with act.Fori(0, WINDOWS) as w:
                        act.wait_ge(sems.rows_here[0], (g + 1) * (16 * TILES))
                        act.wait_ge(sems.added, g * WINDOWS + w + 1)
                        for t in range(TILES):
                            last = nc.scalar.activation(
                                select[:, 0, t, :], att_rows[:, bass.ds(w * WINDOW, WINDOW)],
                                ACT.Sigmoid, bias=gathered[:, 0, t, FEAT:MSG_ROW])
                        last.then_inc(sems.sigmoids_ready, 1)
            by_case(act, sigmoids_layer1, sigmoids_all)

            def gates(j, half):
                act.wait_ge(gates_mm, j + 1)
                for gate in range(2):
                    nc.scalar.activation(gru[:, half, gate, :], psum[:, 4 * half + gate, 0:CHUNK],
                                         ACT.Sigmoid, bias=gate_bias[:, gate:gate + 1]).then_inc(rz_ready, 1)
                act.wait_ge(n_input, j + 1)
                nc.scalar.activation(gru[:, half, 3, :], gru[:, half, 2, :], ACT.Tanh, bias=b_ih_c[:, 2:3])\
                  .then_inc(n_ready, 1)
            with act.Fori(0, CHUNKS // 2) as r:
                for half in range(2):
                    gates(r * 2 + half, half)

            act.wait_ge(bn_step, 1)
            nc.scalar.activation(bn[:, 2:3], bn[:, 1:2], ACT.Sqrt, bias=eps[:, 0:1]).then_inc(bn_std, 1)

            act.wait_ge(bn_ready, 1)

            def scale_h(i, r, s):
                act.wait_ge(y_block, i + 1)
                nc.scalar.activation(block_slots[:, s % 2, :], sums_t[:, columns(i, P)], ACT.Identity,
                                     bias=bn[:, 6:7], scale=bn[:, 4:5]).then_inc(y_scaled, 1)
                act.wait_ge(y_turned, i + 3)
                nc.scalar.activation(node_rows[:, columns(i, P)], psum[:, s % 2, 0:P], ACT.Copy)\
                  .then_inc(y_copied, 1)
            over_blocks(act, scale_h)

            act.wait_ge(norm_step[1], 5)
            nc.scalar.activation(norm[:, 5, :], norm[:, 4, :], ACT.Sqrt, bias=eps[:, 0:1])\
              .then_inc(std_ready[1], 1)

        @block.tensor
        def _(pe):
            pe.sem_inc(rel_mm, 2)
            pe.sem_inc(x_turned, 4)
            pe.sem_inc(sum_turned, 2)
            pe.sem_inc(x1_turned, 2)
            pe.sem_inc(msg_mm, 2)
            pe.sem_inc(y_turned, 2)
            pe.sem_inc(one_window.summed, 2)
            pe.sem_inc(hot_used, HOT_SLOTS)
            pe.sem_inc(factors_used, CHUNK_BLOCKS)

            pe.wait_ge(ident_made, 2)
            pe.wait_ge(consts_made, 4)
            pe.wait_ge(diag_ready, 2)
            for n in range(2):
                last = nc.tensor.matmul(psum[:, 7, n * GROUPS:(n + 1) * GROUPS], ones[0:GROUPS, :],
                                        diag[0:GROUPS, n, :], start=True, stop=True)
            last.then_inc(base_spread, 1)

            pe.wait_ge(weights_here, 13 * 16)
            for gate in range(3):
                nc.tensor.transpose(psum[:, 5, gate * P:(gate + 1) * P], w_ih_rows[:, gate, :], ident[:, :])
                last = nc.tensor.transpose(psum[:, 6, gate * P:(gate + 1) * P], w_hh_rows[:, gate, :],
                                           ident[:, :])
            last.then_inc(gates_turned, 1)

            pe.wait_ge(planes_ready, 1)
            planes = (raw_dst, raw_weight, raw_key, raw_lo, raw_type, raw_src)
            for t in range(TILES):
                if t >= 2:
                    pe.wait_ge(words_act, t - 1)
                    pe.wait_ge(words_dve, t - 1)
                for w, plane in enumerate(planes):
                    last = nc.tensor.transpose(psum[:, t % 2 + 2 * (w // 4), (w % 4) * P:(w % 4) * P + GROUPS],
                                               plane[0:GROUPS, t * P:(t + 1) * P],
                                               ident[0:GROUPS, 0:GROUPS])
                last.then_inc(edges_turned, 1)

            def turn_x(i, r, s):
                pe.wait_ge(x_here[s], (r + 1) * 16)
                pe.wait_ge(xt_copied, i + 1)
                nc.tensor.transpose(psum[:, 2 + s % 2, 0:P], x_slots[:, s, :], ident[:, :])\
                  .then_inc(x_turned, 1)

            def multiply_x(i, r, s):
                pe.wait_ge(xt_copied, i + 3)
                pe.wait_ge(rel_act, i + 1)
                pe.wait_ge(rel_dve, i + 1)
                for half in range(2):
                    last = nc.tensor.matmul(psum[:, 4 + 2 * (s % 2) + half, :], block_slots[:, s % 2, :],
                                            rel_w[:, 4 * half:4 * half + 4, :].rearrange("p r o -> p (r o)"),
                                            start=True, stop=True)
                last.then_inc(rel_mm, 1)
            pe.wait_ge(words_act, TILES)
            pe.wait_ge(words_dve, TILES)
            pe.wait_ge(gates_copied, 1)
            pe.wait_ge(base_ready, 1)
            turn_x(0, 0, 0)

            def both(i, r, s):
                turn_x(i + 1, r + (s + 1) // 4, (s + 1) % 4)
                multiply_x(i, r, s)
            with pe.Fori(0, (BLOCKS - 1) // 4) as r:
                for s in range(4):
                    both(r * 4 + s, r, s)
            multiply_x(BLOCKS - 1, (BLOCKS - 1) // 4, 0)

            def sum_group(s, half, bank, sems):
                for t in range(TILES):
                    last = nc.tensor.matmul(psum[:, bank, 0:WINDOW], gathered[:, s, t, 0:FEAT],
                                            select[:, half, t, :], start=(t == 0), stop=(t == TILES - 1))
                last.then_inc(sems.summed, 1)

            def products_layer0():
                sems = one_window
                with pe.Fori(0, ROUNDS) as r:
                    for s in range(SLOTS):
                        g = r * SLOTS + s
                        pe.wait_ge(sems.rows_here[s], (r + 1) * (16 * TILES))
                        pe.wait_ge(sems.added, g + SLOTS)
                        pe.wait_ge(sems.select_ready, g + 3)
                        sum_group(s, s % 2, 0, sems)
                        pe.wait_ge(counts_out, g + 1)
                        for t in range(TILES):
                            pe.wait_ge(hot_ready, g * TILES + t + 1)
                            count_tile(t, (s * TILES + t) % HOT_SLOTS)

            def count_tile(t, slot):
                for c in range(BANKS):
                    blocks = min(BANK_BLOCKS, BLOCKS - c * BANK_BLOCKS)
                    to = psum[:, 1 + c, 0:BANK_COLS].rearrange("p (h w) -> p h w", h=BANK_BLOCKS)
                    keys = slice(c * BANK_BLOCKS * TILE_WINDOW, (c * BANK_BLOCKS + blocks) * TILE_WINDOW)
                    last = nc.tensor.matmul(
                        to[:, 0:blocks, TILE_START[t]:TILE_START[t] + TILE_WINDOW], lo_hot[:, slot, :],
                        key_hot[:, slot, keys].rearrange("p (h w) -> p h w", h=blocks),
                        start=(t == 0), stop=(t == TILES - 1), skip_group_check=True)
                last.then_inc(hot_used, 1)

            def products_layer1():
                pe.wait_ge(msg_biased, BLOCKS + 4)

                def multiply(k, turn, parity, groups):
                    pe.wait_ge(panel_added, k * PANEL + 1)
                    for b in range(BLOCKS):
                        pe.wait_ge(factors_ready, (k + 1) * BLOCKS + b + 1)
                        nc.tensor.matmul(psum[:, parity, 0:groups * WINDOW], msg_rows[:, b, 0:FEAT],
                                         factors[:, b % CHUNK_BLOCKS, 0:groups * WINDOW],
                                         start=(b == 0), stop=(b == BLOCKS - 1)).then_inc(factors_used, 1)
                over_panels(pe, multiply)

            def sum_all(layer):
                sems = all_windows[layer]

                def run():
                    with pe.Fori(0, GROUPS) as g:
                        with pe.Fori(0, WINDOWS) as w:
                            pe.wait_ge(sems.rows_here[0], (g + 1) * (16 * TILES))
                            pe.wait_ge(sems.select_ready, g * WINDOWS + w + 1)
                            sum_group(0, 0, 0, sems)
                return run
            by_case(pe, products_layer0, sum_all(0))

            def turn_sums(i, r, s):
                pe.wait_ge(sum_block, i + 1)
                pe.wait_ge(rows_added, i + 3)
                nc.tensor.transpose(psum[:, s % 2, 0:P], block_slots[:, s % 2, :], ident[:, :])\
                  .then_inc(sum_turned, 1)
            over_blocks(pe, turn_sums)

            def turn_x1(i, r, s):
                pe.wait_ge(x1_block, i + 1)
                pe.wait_ge(x1_copied, i + 1)
                nc.tensor.transpose(psum[:, s % 2, 0:P], block_slots[:, s % 2, :], ident[:, :])\
                  .then_inc(x1_turned, 1)
            over_blocks(pe, turn_x1)

            def multiply_x1(i, r, s):
                pe.wait_ge(x1_slot, i + 1)
                pe.wait_ge(msg_biased, i + 3)
                nc.tensor.matmul(psum[:, 2 + s % 2, 0:MSG_ALL], block_slots2[:, s % 2, :], table_w[:, :],
                                 start=True, stop=True).then_inc(msg_mm, 1)
            over_blocks(pe, multiply_x1)

            pe.wait_ge(rep_ready, 1)
            with pe.Fori(0, CHUNKS) as j:
                pe.wait_ge(att_copied, j + 1)
                nc.tensor.matmul(psum[:, 4, 0:CHUNK], att_dst_rep[:, :], nodes_t[:, bass.ds(j * CHUNK, CHUNK)],
                                 start=True, stop=True).then_inc(att_mm, 1)

            by_case(pe, products_layer1, sum_all(1))

            pe.wait_ge(sweep_done[1], 1)

            def gate_products(j, half):
                pe.wait_ge(h_ready, j + 1)
                cols = bass.ds(j * CHUNK, CHUNK)
                for gate in range(2):
                    nc.tensor.matmul(psum[:, 4 * half + gate, 0:CHUNK], w_ih_t[:, gate, :], sums_t[:, cols],
                                     start=True, stop=False)
                    nc.tensor.matmul(psum[:, 4 * half + gate, 0:CHUNK], w_hh_t[:, gate, :], nodes_t[:, cols],
                                     start=False, stop=True)
                nc.tensor.matmul(psum[:, 4 * half + 2, 0:CHUNK], w_ih_t[:, 2, :], sums_t[:, cols],
                                 start=True, stop=True)
                nc.tensor.matmul(psum[:, 4 * half + 3, 0:CHUNK], w_hh_t[:, 2, :], nodes_t[:, cols],
                                 start=True, stop=True).then_inc(gates_mm, 1)
            with pe.Fori(0, CHUNKS // 2) as r:
                for half in range(2):
                    gate_products(r * 2 + half, half)

            def turn_y(i, r, s):
                pe.wait_ge(y_block, i + 3)
                pe.wait_ge(y_copied, i + 1)
                nc.tensor.transpose(psum[:, s % 2, 0:P], block_slots2[:, s % 2, :], ident[:, :])\
                  .then_inc(y_turned, 1)
            over_blocks(pe, turn_y)

        @block.vector
        def _(dve):
            v = nc.vector
            dve.sem_inc(xt_copied, 2)
            dve.sem_inc(rel_dve, 2)
            dve.sem_inc(rows_added, 4)
            dve.sem_inc(msg_biased, 4)
            dve.sem_inc(att_copied, 1)
            dve.sem_inc(h_ready, 2)
            dve.sem_inc(y_block, 2)
            dve.sem_inc(y_copied, 2)
            dve.sem_inc(one_window.select_ready, 2)
            dve.sem_inc(one_window.added, SLOTS)
            dve.sem_inc(factors_ready, BLOCKS)
            dve.sem_inc(panel_added, 1)
            for layer in range(2):
                dve.sem_inc(all_windows[layer].added, 1)

            tail = slice(LAST_EDGES, GROUP)
            v.memset(table_bias[:, MSG_ROW:MSG_ALL], 0.0).then_inc(bias_clear, 1)
            v.memset(raw_dst_big.bitcast(I32)[96:P, tail], 1 << 20).then_inc(pads_set, 1)
            v.memset(raw_dst.bitcast(I32)[96:P, tail], int(NO_MATCH)).then_inc(pads_set, 1)
            v.memset(raw_src[96:P, tail], 0.0).then_inc(pads_set, 1)
            v.memset(raw_type[96:P, tail], 0.0).then_inc(pads_set, 1)
            v.memset(raw_weight[96:P, tail], 0.0).then_inc(pads_set, 1)
            dve.wait_ge(consts_made, 4)
            v.tensor_copy(window_iota[:, :], window_iota_i[:, :]).then_inc(consts_cast, 1)
            v.tensor_copy(window_start[:, :], window_start_i[:, :]).then_inc(consts_cast, 1)

            dve.wait_ge(key_iota_made, 1)
            v.tensor_copy(key_iota, key_iota_i).then_inc(consts_cast, 1)

            g = slice(0, GROUPS)
            steps = [0]

            def step(*instructions):
                for instruction in instructions:
                    instruction.then_inc(prep_step, 1)
                steps[0] += len(instructions)
                dve.wait_ge(prep_step, steps[0])

            def tiles(raw):
                return raw[g, :].rearrange("g (t e) -> g t e", t=TILES)
            starts = tile_starts[g, :]
            dve.wait_ge(raw_here, 10 * 16)
            dve.wait_ge(starts_made, 1)
            step(v.tensor_reduce(lo[g, 0:TILES], tiles(raw_dst_big.bitcast(I32)), AX.X, ALU.min),
                 v.tensor_reduce(hi[g, :], tiles(raw_dst.bitcast(I32)), AX.X, ALU.max))
            step(v.tensor_reduce(lo[g, TILES:TILES + 1], lo[g, 0:TILES], AX.X, ALU.min),
                 v.tensor_sub(hi[g, :], hi[g, :], starts),
                 v.tensor_sub(low_miss[g, :], starts, lo[g, 0:TILES]))
            group_lo = lo[g, TILES:TILES + 1]
            step(v.tensor_scalar(hi[g, :], hi[g, :], group_lo, float(TILE_WINDOW - 1), ALU.subtract, ALU.subtract),
                 v.tensor_scalar(low_miss[g, :], low_miss[g, :], group_lo, None, ALU.add))
            step(v.tensor_tensor(miss[g, 0:TILES], hi[g, :], low_miss[g, :], ALU.max))
            step(v.tensor_reduce(miss[g, TILES:TILES + 1], miss[g, 0:TILES], AX.X, ALU.max))
            dve.wait_ge(ident_made, 2)
            v.tensor_scalar(diag[g, 0, :], ident[g, g], group_lo, None, ALU.mult).then_inc(diag_ready, 1)
            v.tensor_scalar(diag[g, 1, :], ident[g, g], miss[g, TILES:TILES + 1], None, ALU.mult)\
             .then_inc(diag_ready, 1)

            step(v.tensor_scalar(raw_lo.bitcast(I32)[g, :], raw_src.bitcast(I32)[g, :], P - 1, None,
                                 ALU.bitwise_and),
                 v.tensor_scalar(raw_key.bitcast(I32)[g, :], raw_src.bitcast(I32)[g, :], 7, None,
                                 ALU.arith_shift_right))
            step(v.tensor_copy(raw_lo[g, :], raw_lo.bitcast(I32)[g, :]),
                 v.tensor_copy(raw_src[g, :], raw_src.bitcast(I32)[g, :]),
                 v.tensor_copy(raw_dst[g, :], raw_dst.bitcast(I32)[g, :]))
            step(v.scalar_tensor_tensor(raw_type[g, :], raw_src[g, :], float(RELS), raw_type.bitcast(I32)[g, :],
                                        ALU.mult, ALU.add))
            dve.wait_ge(base_spread, 1)
            step(v.tensor_reduce(case[:, 0:1], psum[:, 7, GROUPS:2 * GROUPS], AX.X, ALU.max))
            step(v.tensor_scalar(case[:, 1:2], case[:, 0:1], 0.0, None, ALU.is_le),
                 v.tensor_scalar(case[:, 0:1], case[:, 0:1], 0.0, None, ALU.is_gt))
            dve.wait_ge(base_clear, 1)
            step(v.tensor_mul(group_base[g, :], group_lo, case[g, 1:2]),
                 v.tensor_copy(case_i[:, :], case[:, 0:1]),
                 v.tensor_scalar(base_row[:, PANEL:PANEL + GROUPS], psum[:, 7, 0:GROUPS], case[:, 1:2], None, ALU.mult))
            step(v.tensor_scalar(raw_dst[g, :], raw_dst[g, :], group_base[g, :], None, ALU.subtract))
            step(v.scalar_tensor_tensor(raw_key[g, :], raw_key.bitcast(I32)[g, :], float(TILE_WINDOW),
                                        raw_dst[g, :], ALU.mult, ALU.add))
            v.tensor_sub(tiles(raw_key), tiles(raw_key),
                         starts.rearrange("g (t e) -> g t e", e=1).broadcast_to((GROUPS, TILES, P)))\
             .then_inc(planes_ready, 1)
            dve.drain().then_inc(base_ready, 1)

            dve.wait_ge(gates_turned, 1)
            v.tensor_copy(w_ih_t[:, :, :].rearrange("p g o -> p (g o)"), psum[:, 5, 0:3 * P])
            v.tensor_copy(w_hh_t[:, :, :].rearrange("p g o -> p (g o)"), psum[:, 6, 0:3 * P])
            v.tensor_add(gate_bias[:, :], b_ih_c[:, 0:2], b_hh_c[:, 0:2])
            v.tensor_scalar(att_dst_rep[:, :], ones[:, :], att_dst[:, 0:1], None, ALU.mult)\
             .then_inc(rep_ready, 1)
            dve.drain().then_inc(gates_copied, 1)

            for t in range(TILES):
                dve.wait_ge(edges_turned, t + 1)
                v.tensor_copy(edge_words[:, :, 0:ROWS_WORD, t].rearrange("p g w -> p w g").bitcast(F32),
                              psum[:, t % 2, :].rearrange("p (w g) -> p w g", w=ROWS_WORD)[:, :, 0:GROUPS])\
                 .then_inc(words_dve, 1)

            def copy_xt(i, r, s):
                dve.wait_ge(x_turned, i + 5)
                dve.wait_ge(rel_mm, i + 1)
                v.tensor_copy(block_slots[:, s % 2, :], psum[:, 2 + s % 2, 0:P]).then_inc(xt_copied, 1)

            def evacuate(i, r, s):
                dve.wait_ge(rel_mm, i + 3)
                dve.wait_ge(rel_stored[s], (r + 1) * 16)
                v.tensor_copy(table_slots[:, s, 512:1024], psum[:, 5 + 2 * (s % 2), :]).then_inc(rel_dve, 1)
            copy_xt(0, 0, 0)
            with dve.Fori(0, (BLOCKS - 1) // 4) as r:
                for s in range(4):
                    copy_xt(r * 4 + s + 1, r + (s + 1) // 4, (s + 1) % 4)
                    evacuate(r * 4 + s, r, s)
            evacuate(BLOCKS - 1, (BLOCKS - 1) // 4, 0)

            def select_tile(layer, t, s, half, places):
                if layer == 0:
                    return v.tensor_scalar(select[:, half, t, :], window_iota[:, :], places[:, t:t + 1],
                                           words_f[:, s, 1, t:t + 1], ALU.is_equal, ALU.mult)
                return v.scalar_tensor_tensor(select[:, half, t, :], window_iota[:, :], places[:, t:t + 1],
                                              select[:, half, t, :], ALU.is_equal, ALU.mult)

            def add_window(entry, columns_from, added, done):
                base = dve.value_load(base_row[0:1, bass.ds(entry, 1)], min_val=0, max_val=NODES - 1)
                dve.wait_ge(added, done)
                to = sums_t[:, bass.ds(base, WINDOW)]
                v.tensor_add(to, to, columns_from).then_inc(added, 1)

            def layer0():
                sems = one_window
                with dve.Fori(0, ROUNDS) as r:
                    for s in range(SLOTS):
                        g = r * SLOTS + s
                        dve.wait_ge(sems.words_here[s], (r + 1) * 16)
                        dve.wait_ge(sems.summed, g + 1)
                        for t in range(TILES):
                            last = select_tile(0, t, s, s % 2, words_f[:, s, 0, :])
                        last.then_inc(sems.select_ready, 1)
                        for t in range(TILES):
                            slot = (s * TILES + t) % HOT_SLOTS
                            dve.wait_ge(hot_used, g * TILES + t + 1)
                            v.tensor_scalar(key_hot[:, slot, :], key_iota, words_f[:, s, 2, t:t + 1],
                                            None, ALU.is_equal)
                            v.tensor_scalar(lo_hot[:, slot, :], key_iota[:, 0:P],
                                            words_f[:, s, 3, t:t + 1], None, ALU.is_equal).then_inc(hot_ready, 1)
                        dve.wait_ge(sems.summed, g + 3)
                        add_window(g + PANEL, psum[:, 0, 0:WINDOW], sems.added, g + SLOTS)

            def layer1():
                v.memset(psum[:, 1, 0:PANEL_COLS], 0.0).then_inc(sums_clear, 1)
                dve.wait_ge(sums_clear, 3)

                def scale(k, turn, parity, groups):
                    for b in range(BLOCKS):
                        c = b // CHUNK_BLOCKS
                        factor = factors[:, b % CHUNK_BLOCKS, 0:groups * WINDOW]\
                            .rearrange("p (g w) -> p g w", g=groups)
                        cols = slice(b % CHUNK_BLOCKS * WINDOW, (b % CHUNK_BLOCKS + 1) * WINDOW)
                        if b % CHUNK_BLOCKS == 0:
                            dve.wait_ge(counts_here[c], (k + 1) * 16)
                        dve.wait_ge(sigmoids_ready, (k + 2) * BLOCKS + b + 1)
                        v.tensor_mul(factor, factor, counts[:, c, 0:groups, cols]).then_inc(factors_ready, 1)
                        if b in range(3, 3 + 2 * PANEL, 2):
                            add_before(k, (b - 3) // 2, 1 - parity)

                def add_before(k, i, bank):
                    if i == 0:
                        dve.wait_ge(factors_used, k * BLOCKS + CHUNK_BLOCKS)
                    add_window(k * PANEL + i, psum[:, bank, i * WINDOW:(i + 1) * WINDOW], panel_added,
                               k * PANEL + i + 1)
                over_panels(dve, scale)
                for i in range(LAST_PANEL):
                    add_before(PANELS, i, 1)

            def sweep_all(layer):
                sems = all_windows[layer]

                def run():
                    with dve.Fori(0, GROUPS) as g:
                        with dve.Fori(0, WINDOWS) as w:
                            dve.wait_ge(sems.words_here[0], (g + 1) * 16)
                            done = g * WINDOWS + w
                            dve.wait_ge(sems.added, done + 1)
                            v.tensor_scalar(in_window[:, :], words_f[:, 0, 0, :],
                                            window_start[:, bass.ds(w, 1)], None, ALU.subtract)\
                             .then_inc(sems.shifted, 1)
                            dve.wait_ge(sems.shifted, done + 1)
                            if layer == 1:
                                dve.wait_ge(sems.sigmoids_ready, done + 1)
                            for t in range(TILES):
                                last = select_tile(layer, t, 0, 0, in_window)
                            last.then_inc(sems.select_ready, 1)
                            dve.wait_ge(sems.summed, done + 1)
                            to = sums_t[:, bass.ds(w * WINDOW, WINDOW)]
                            v.tensor_add(to, to, psum[:, 0, 0:WINDOW]).then_inc(sems.added, 1)
                return run

            dve.wait_ge(consts_cast, 3)
            dve.wait_ge(sums_clear, 1)
            by_case(dve, layer0, sweep_all(0))
            dve.drain().then_inc(sweep_done[0], 1)

            def add_rows(i, r, s):
                dve.wait_ge(xa_here[s], (r + 1) * 16)
                dve.wait_ge(sum_turned, i + 3)
                v.tensor_add(node_rows[:, columns(i, P)], x_slots[:, s, :], psum[:, s % 2, 0:P])\
                 .then_inc(rows_added, 1)
                dve.wait_ge(rows_added, i + 5)
                v.bn_stats(stats[:, columns(i, 1), :].rearrange("p i s -> p (i s)"),
                           node_rows[:, columns(i, P)]).then_inc(stats_ready[0], 1)
            over_blocks(dve, add_rows)

            def normalisers(n):
                sems = norm_step[n]
                dve.wait_ge(stats_ready[n], BLOCKS)
                v.tensor_add(norm[:, 1, :], stats[:, :, 1], stats[:, :, 4]).then_inc(sems, 1)
                v.tensor_sub(norm[:, 2, :], stats[:, :, 1], stats[:, :, 4]).then_inc(sems, 1)
                v.tensor_add(norm[:, 3, :], stats[:, :, 2], stats[:, :, 5]).then_inc(sems, 1)
                dve.wait_ge(sems, 3)
                v.tensor_scalar(norm[:, 0, :], norm[:, 1, :], 0.5, None, ALU.mult)
                v.tensor_scalar(norm[:, 3, :], norm[:, 3, :], 1.0 / FEAT, None, ALU.mult)
                v.scalar_tensor_tensor(norm[:, 7, :], norm[:, 2, :], 0.25, norm[:, 2, :], ALU.mult, ALU.mult)\
                 .then_inc(sems, 1)
                dve.wait_ge(sems, 4)
                v.tensor_add(norm[:, 4, :], norm[:, 7, :], norm[:, 3, :]).then_inc(sems, 1)
                dve.wait_ge(std_ready[n], 1)
                v.reciprocal(norm[:, 6, :], norm[:, 5, :]).then_inc(sems, 1)
                dve.wait_ge(sems, 6)
            normalisers(0)

            def x1_rows(i, r, s):
                dve.wait_ge(x1_turned, i + 1)
                v.tensor_scalar(block_slots[:, s % 2, :], node_rows[:, columns(i, P)],
                                norm[:, 0, columns(i, 1)], norm[:, 6, columns(i, 1)],
                                ALU.subtract, ALU.mult).then_inc(x1_block, 1)
            over_blocks(dve, x1_rows)

            def bias_messages(i, r, s):
                dve.wait_ge(msg_mm, i + 3)
                v.tensor_add(msg_block(i), psum[:, 2 + s % 2, 0:MSG_ALL], table_bias[:, :])\
                 .then_inc(msg_biased, 1)
            over_blocks(dve, bias_messages)
            v.memset(att_rows[:, PADDED:SUM_COLS], 0.0).then_inc(att_end_clear, 1)

            dve.wait_ge(sums_clear, 2)
            by_case(dve, layer1, sweep_all(1))
            dve.drain().then_inc(sweep_done[1], 1)

            def update(j, half, valid):
                cols = bass.ds(j * CHUNK, CHUNK)
                slot = gru[:, half, :, :]
                dve.wait_ge(rz_ready, j * 2 + 2)
                v.scalar_tensor_tensor(slot[:, 4, :], psum[:, 4 * half + 3, 0:CHUNK], b_hh_c[:, 2:3],
                                       slot[:, 0, :], ALU.add, ALU.mult).then_inc(n_step, 1)
                dve.wait_ge(n_step, j + 1)
                v.tensor_add(slot[:, 2, :], slot[:, 4, :], psum[:, 4 * half + 2, 0:CHUNK]).then_inc(n_input, 1)
                dve.wait_ge(n_ready, j + 1)
                v.tensor_sub(slot[:, 5, :], nodes_t[:, cols], slot[:, 3, :]).then_inc(h_step, 1)
                dve.wait_ge(h_step, j * 2 + 1)
                v.tensor_mul(slot[:, 5, :], slot[:, 5, :], slot[:, 1, :]).then_inc(h_step, 1)
                dve.wait_ge(h_step, j * 2 + 2)
                v.tensor_add(sums_t[:, cols], slot[:, 5, :], slot[:, 3, :]).then_inc(h_ready, 1)
                dve.wait_ge(h_ready, j + 3)
                v.bn_stats(bn_stats[:, columns(j, 1), :].rearrange("p i s -> p (i s)"),
                           sums_t[:, bass.ds(j * CHUNK, valid)]).then_inc(h_stats, 1)
            with dve.Fori(0, CHUNKS // 2 - 1) as r:
                for half in range(2):
                    update(r * 2 + half, half, CHUNK)
            update(CHUNKS - 2, 0, CHUNK)
            update(CHUNKS - 1, 1, NODES - (CHUNKS - 1) * CHUNK)

            dve.wait_ge(h_stats, CHUNKS)
            v.bn_aggr(bn[:, 0:2], bn_stats[:, :, :].rearrange("p j s -> p (j s)")).then_inc(bn_step, 1)
            dve.wait_ge(bn_std, 1)
            v.reciprocal(bn[:, 3:4], bn[:, 2:3]).then_inc(bn_step, 1)
            dve.wait_ge(bn_step, 2)
            v.tensor_mul(bn[:, 4:5], bn[:, 3:4], gamma_c[:, :]).then_inc(bn_step, 1)
            dve.wait_ge(bn_step, 3)
            v.tensor_mul(bn[:, 5:6], bn[:, 0:1], bn[:, 4:5]).then_inc(bn_step, 1)
            dve.wait_ge(bn_step, 4)
            v.tensor_sub(bn[:, 6:7], beta_c[:, :], bn[:, 5:6]).then_inc(bn_ready, 1)

            def add_y(i, r, s):
                dve.wait_ge(y_scaled, i + 1)
                dve.wait_ge(y_turned, i + 1)
                v.tensor_add(block_slots2[:, s % 2, :], block_slots[:, s % 2, :], nodes_t[:, columns(i, P)])\
                 .then_inc(y_block, 1)
                dve.wait_ge(y_copied, i + 3)
                v.bn_stats(stats[:, columns(i, 1), :].rearrange("p i s -> p (i s)"), node_rows[:, columns(i, P)])\
                 .then_inc(y_stats, 1)
            over_blocks(dve, add_y)
            dve.wait_ge(y_stats, BLOCKS)
            dve.drain().then_inc(stats_ready[1], BLOCKS)
            dve.wait_ge(y_copied, BLOCKS + 2)
            normalisers(1)

            def out_rows(i, r, s):
                dve.wait_ge(out_stored[s], (r + 1) * 16)
                v.tensor_scalar(out_slots[:, s, 0:FEAT], node_rows[:, columns(i, P)],
                                norm[:, 0, columns(i, 1)], norm[:, 6, columns(i, 1)],
                                ALU.subtract, ALU.mult).then_inc(out_ready, 1)
            over_blocks(dve, out_rows)


INPUTS = ["x", "src", "dst", "edge_type_8", "edge_weight", "L0_gnn_rel_emb", "L1_gnn_W_msg",
          "L1_gnn_b_msg", "L1_gnn_W_att", "L1_gnn_b_att", "L1_gnn_W_ih", "L1_gnn_b_ih",
          "L1_gnn_W_hh", "L1_gnn_b_hh", "L1_gnn_gamma", "L1_gnn_beta"]


def kernel(**inputs):
    import numpy as np
    import concourse.bacc as bacc
    from concourse import mybir as mb
    from concourse.bass_utils import run_bass_kernel_spmd

    nc = bacc.Bacc("TRN2", target_bir_lowering=False, num_devices=1)
    arrays, args = {}, []
    for name in INPUTS:
        a = np.ascontiguousarray(inputs[name])
        arrays[f"in_{name}"] = a
        args.append(nc.dram_tensor(f"in_{name}", a.shape, mb.dt.from_np(a.dtype), kind="ExternalInput").ap())
    out = nc.dram_tensor("out", (NODES, FEAT), F32, kind="ExternalOutput").ap()
    build(nc, *args, out)
    result = run_bass_kernel_spmd(nc, [arrays], core_ids=[0])
    return result.results[0]["out"]
```

```python
import concourse.bass as bass
from concourse import mybir
from contextlib import ExitStack

F32 = mybir.dt.float32
I32 = mybir.dt.int32
F16 = mybir.dt.float16
U32 = mybir.dt.uint32
ALU = mybir.AluOpType
ACT = mybir.ActivationFunctionType
AX = mybir.AxisListType

P = 128
NODES = 6250
FEAT = 128
RELS = 8
EDGES = 206250
EPS = 1e-5

TILES = 13
GROUP = TILES * P
GROUPS = -(-EDGES // GROUP)
LAST_EDGES = EDGES - (GROUPS - 1) * GROUP
SLOTS = 4
ROUNDS = GROUPS // SLOTS
WINDOW = 58
WINDOWS = -(-NODES // WINDOW)
BLOCKS = -(-NODES // P)
LAST_ROWS = NODES - (BLOCKS - 1) * P
PADDED = BLOCKS * P
SUM_COLS = PADDED + WINDOW
CHUNK = 448
CHUNKS = PADDED // CHUNK
MSG_ROW = FEAT + 1
MSG_ALL = FEAT + 2
PANEL = 8
PANELS = -(-GROUPS // PANEL)
LAST_PANEL = GROUPS - (PANELS - 1) * PANEL
CHUNK_BLOCKS = 7
COUNT_CHUNKS = BLOCKS // CHUNK_BLOCKS
BANK_BLOCKS = 8
BANKS = -(-BLOCKS // BANK_BLOCKS)
BANK_COLS = BANK_BLOCKS * WINDOW
PANEL_COLS = PANEL * WINDOW
TILE_WINDOW = 16
KEYS = BLOCKS * TILE_WINDOW
TILE_START = [min(max(round(P * NODES / EDGES * t) - 5, 0), WINDOW - TILE_WINDOW) for t in range(TILES)]
HOT_SLOTS = 4
WORDS = 6
ROWS_WORD = 4
COUNT_COLS = BLOCKS * WINDOW
NO_MATCH = -1.0
REL_TURN = 8
REL_TURNS = (BLOCKS - 1) // REL_TURN
BASE_TURN = 1
WORDS_TURN = 2
WORD_STORES = 4
QUAD = 4
QUAD_COLS = QUAD * P
QUADS = -(-BLOCKS // QUAD)
X1_BATCHES = ((0, 5), (5, 9), (9, QUADS))
AHEAD = X1_BATCHES[0][1]
OUT_BATCHES = ((0, 4), (4, 8), (8, 11), (11, QUADS))
assert TILE_START[-1] + TILE_WINDOW == WINDOW and PANELS % 2 == 0 and COUNT_CHUNKS * CHUNK_BLOCKS == BLOCKS
assert GROUPS % WORD_STORES == 0 and REL_TURNS * REL_TURN + 1 == BLOCKS and (BLOCKS - 1) % 4 == 0
assert ROUNDS * SLOTS == GROUPS and CHUNKS * CHUNK == PADDED


def build(nc, x, src, dst, edge_type, edge_weight, rel_emb, w_msg, b_msg, w_att, b_att, w_ih, b_ih,
          w_hh, b_hh, gamma, beta, out):
    ctx = ExitStack()
    with ctx:
        def sb(name, shape, dt=F32):
            return ctx.enter_context(nc.sbuf_tensor(name, shape, dt))

        def sem(name):
            return ctx.enter_context(nc.semaphore(name))

        rel_table = nc.dram_tensor("rel_table", (NODES, RELS * FEAT), F32, kind="Internal").ap()
        rel_table_rows = rel_table.rearrange("n (r f) -> (n r) f", r=RELS)
        count_table = nc.dram_tensor("count_table", (GROUPS, P, COUNT_COLS), F16, kind="Internal").ap()
        edge_table = nc.dram_tensor("edge_table", (P, GROUPS * WORDS * TILES), I32, kind="Internal").ap()
        msg_table = nc.dram_tensor("msg_table", (NODES, MSG_ROW), F32, kind="Internal").ap()

        ident = sb("ident", [P, P])
        ones = sb("ones", [P, P])
        window_iota_i = sb("window_iota_i", [P, WINDOW], I32)
        window_iota = sb("window_iota", [P, WINDOW])
        window_start_i = sb("window_start_i", [P, WINDOWS], I32)
        window_start = sb("window_start", [P, WINDOWS])
        eps = sb("eps", [P, 1])
        rel_w = sb("rel_w", [P, RELS, FEAT])
        table_w = sb("table_w", [P, MSG_ALL])
        table_bias = sb("table_bias", [P, MSG_ALL])
        att_dst = sb("att_dst", [P, 1])
        att_dst_rep = sb("att_dst_rep", [P, P])
        w_ih_t = sb("w_ih_t", [P, 3, P])
        w_hh_t = sb("w_hh_t", [P, 3, P])
        b_ih_c = sb("b_ih_c", [P, 3])
        b_hh_c = sb("b_hh_c", [P, 3])
        gate_bias = sb("gate_bias", [P, 2])
        gamma_c = sb("gamma_c", [P, 1])
        beta_c = sb("beta_c", [P, 1])

        node_space = sb("node_space", [P, PADDED + SUM_COLS])
        nodes_t = node_space[:, 0:PADDED]
        sums_t = node_space[:, PADDED:]
        att_rows = sb("att_rows", [P, SUM_COLS])
        row_space = sb("row_space", [P, BLOCKS * MSG_ALL])
        node_rows = row_space[:, 0:PADDED]
        msg_rows = row_space[:, :].rearrange("p (b m) -> p b m", b=BLOCKS)
        stage_space = sb("stage_space", [P, COUNT_CHUNKS * CHUNK_BLOCKS * PANEL_COLS // 2])
        gather_space = stage_space[:, 0:SLOTS * TILES * MSG_ROW]
        gathered = gather_space.rearrange("p (s t m) -> p s t m", s=SLOTS, t=TILES)
        counts_out_slots = stage_space[:, SLOTS * TILES * MSG_ROW:SLOTS * TILES * MSG_ROW + COUNT_COLS]\
            .bitcast(F16).rearrange("p (s n) -> p s n", s=2)
        counts = stage_space[:, :].bitcast(F16).rearrange("p (c g n) -> p c g n", c=COUNT_CHUNKS, g=PANEL)
        words = sb("words", [P, SLOTS, WORDS, TILES], I32)
        words_f = words[:, :, :, :].bitcast(F32)
        edge_words = node_space[:, 0:GROUPS * WORDS * TILES].bitcast(I32)\
            .rearrange("p (g w t) -> p g w t", g=GROUPS, w=WORDS)
        factors = sb("factors", [P, CHUNK_BLOCKS, PANEL_COLS])
        hot_space = factors[:, :, :].rearrange("p c n -> p (c n)").bitcast(F16)
        key_hot = hot_space[:, 0:HOT_SLOTS * KEYS].rearrange("p (s n) -> p s n", s=HOT_SLOTS)
        lo_hot = hot_space[:, HOT_SLOTS * KEYS:HOT_SLOTS * (KEYS + P)].rearrange("p (s n) -> p s n", s=HOT_SLOTS)
        key_iota = hot_space[:, HOT_SLOTS * (KEYS + P):HOT_SLOTS * (KEYS + P) + KEYS]
        q_panel = sb("q_panel", [P, 2, PANEL_COLS])
        tile_starts = sb("tile_starts", [P, TILES])
        in_window = sb("in_window", [P, TILES])
        select = sb("select", [P, 2, TILES, WINDOW])
        x_slots = sb("x_slots", [P, REL_TURN, FEAT])
        xt_slots = sb("xt_slots", [P, 2, P])
        stats = sb("stats", [P, BLOCKS, 6])
        norm = sb("norm", [P, 8, BLOCKS])
        bn_stats = sb("bn_stats", [P, CHUNKS, 6])
        bn = sb("bn", [P, 8])
        lo = sb("lo", [P, TILES + 1])
        hi = sb("hi", [P, TILES])
        low_miss = sb("low_miss", [P, TILES])
        miss = sb("miss", [P, TILES + 1])
        diag = sb("diag", [P, 2, GROUPS])
        case = sb("case", [P, 2])
        group_base = sb("group_base", [P, 1])
        base_row = sb("base_row", [P, PANEL + GROUPS], I32)
        case_i = sb("case_i", [P, 1], I32)

        x_rows = att_rows[:, 0:PADDED]
        raw_src = att_rows[:, 0:GROUP]
        raw_type = att_rows[:, GROUP:2 * GROUP]
        raw_dst_big = att_rows[:, 2 * GROUP:3 * GROUP]
        raw_key = raw_dst_big
        raw_dst = row_space[:, 0:GROUP]
        raw_weight = row_space[:, GROUP:2 * GROUP]
        raw_lo = row_space[:, 2 * GROUP:3 * GROUP]
        w_rows = gather_space[:, 4 * RELS * FEAT:4 * RELS * FEAT + 6 * FEAT]\
            .rearrange("p (w g f) -> p w g f", w=2, g=3)
        w_ih_rows = w_rows[:, 0, :, :]
        w_hh_rows = w_rows[:, 1, :, :]
        gru = gather_space[:, 0:12 * CHUNK].rearrange("p (s n c) -> p s n c", s=2, n=6)
        key_iota_i = gather_space[:, 5 * RELS * FEAT:5 * RELS * FEAT + KEYS].bitcast(I32)
        assert 5 * RELS * FEAT + KEYS <= SLOTS * TILES * MSG_ROW
        table_slots = gather_space[:, 0:4 * RELS * FEAT]\
            .rearrange("p (s m) -> p s m", s=4)

        psum = ctx.enter_context(nc.psum_tensor("psum", [P, 8, 512], F32))

        pads_set = sem("pads_set")
        dst_here = sem("dst_here")
        src_type_here = sem("src_type_here")
        edge_weights_here = sem("edge_weights_here")
        rel_w_here = sem("rel_w_here")
        weights_here = sem("weights_here")
        ident_made = sem("ident_made")
        consts_made = sem("consts_made")
        consts_cast = sem("consts_cast")
        prep_step = sem("prep_step")
        diag_ready = sem("diag_ready")
        base_spread = sem("base_spread")
        base_ready = sem("base_ready")
        starts_made = sem("starts_made")
        base_clear = sem("base_clear")
        key_iota_made = sem("key_iota_made")
        bias_clear = sem("bias_clear")
        planes_ready = sem("planes_ready")
        edges_turned = sem("edges_turned")
        words_dve = sem("words_dve")
        words_act = sem("words_act")
        words_stored = sem("words_stored")
        gates_turned = sem("gates_turned")
        gates_copied = sem("gates_copied")
        rep_ready = sem("rep_ready")
        x_here = [sem(f"x_here{half}") for half in range(2)]
        x_turned = sem("x_turned")
        xt_copied = sem("xt_copied")
        rel_mm = sem("rel_mm")
        rel_copied = sem("rel_copied")
        rel_stored = [sem(f"rel_stored{s}") for s in range(4)]
        sums_clear = sem("sums_clear")
        bank_clear = sem("bank_clear")
        gathers_begun = sem("gathers_begun")

        class GatherSems:
            def __init__(self, tag, slots):
                self.words_here = [sem(f"words_here_{tag}{s}") for s in range(slots)]
                self.rows_here = [sem(f"rows_here_{tag}{s}") for s in range(slots)]
                self.sigmoids_ready = sem(f"sigmoids_ready_{tag}")
                self.shifted = sem(f"shifted_{tag}")
                self.select_ready = sem(f"select_ready_{tag}")
                self.summed = sem(f"summed_{tag}")
                self.added = sem(f"added_{tag}")

        one_window = GatherSems("one", SLOTS)
        all_windows = [GatherSems(f"all{layer}_", 1) for layer in range(2)]
        hot_ready = sem("hot_ready")
        hot_used = sem("hot_used")
        counts_out = sem("counts_out")
        counts_stored = [sem(f"counts_stored{s}") for s in range(2)]
        counts_here = [sem(f"counts_here{c}") for c in range(COUNT_CHUNKS)]
        q_ready = sem("q_ready")
        sigmoids_ready = sem("sigmoids_ready")
        factors_ready = sem("factors_ready")
        factors_used = sem("factors_used")
        panel_added = sem("panel_added")
        sweep_done = [sem(f"sweep_done{layer}") for layer in range(2)]
        x_pads_clear = sem("x_pads_clear")
        x_rows_here = sem("x_rows_here")
        sums_turned = sem("sums_turned")
        rows_added = sem("rows_added")
        row_stats = sem("row_stats")
        norm_step = [sem(f"norm_step{n}") for n in range(len(X1_BATCHES) + len(OUT_BATCHES))]
        std_ready = [sem(f"std_ready{n}") for n in range(len(X1_BATCHES) + len(OUT_BATCHES))]
        x1_rows_ready = sem("x1_rows_ready")
        x1_turned = sem("x1_turned")
        x1_copied = sem("x1_copied")
        msg_mm = sem("msg_mm")
        msg_copied = sem("msg_copied")
        msg_biased = sem("msg_biased")
        msg_stored = [sem(f"msg_stored{s}") for s in range(4)]
        att_mm = sem("att_mm")
        att_copied = sem("att_copied")
        att_end_clear = sem("att_end_clear")
        gates_mm = sem("gates_mm")
        rz_ready = sem("rz_ready")
        n_input = sem("n_input")
        n_step = sem("n_step")
        n_ready = sem("n_ready")
        h_step = sem("h_step")
        h_ready = sem("h_ready")
        h_stats = sem("h_stats")
        bn_step = sem("bn_step")
        bn_std = sem("bn_std")
        bn_ready = sem("bn_ready")
        y_scaled = sem("y_scaled")
        y_turned = sem("y_turned")
        y_copied = sem("y_copied")
        y_stats = sem("y_stats")
        out_dve = sem("out_dve")
        out_act = sem("out_act")
        out_stored = sem("out_stored")

        block = ctx.enter_context(nc.Block())

        def bank_width(c):
            return min(BANK_BLOCKS, BLOCKS - c * BANK_BLOCKS) * WINDOW

        def over_blocks(engine, body):
            with engine.Fori(0, (BLOCKS - 1) // 4) as r:
                for s in range(4):
                    body(r * 4 + s, r, s)
            body(BLOCKS - 1, (BLOCKS - 1) // 4, 0)

        def quad_blocks(q):
            return range(q * QUAD, min((q + 1) * QUAD, BLOCKS))

        def quad_cols(q):
            return slice(q * QUAD_COLS, min((q + 1) * QUAD_COLS, PADDED))

        def quad_width(q):
            return len(quad_blocks(q)) * P

        def quad_rows(array, q):
            rows = array[q * QUAD_COLS:min((q + 1) * QUAD_COLS, NODES), :]
            blocks = len(quad_blocks(q))
            return rows.rearrange("(b p) f -> p b f", b=blocks), P if blocks > 1 else LAST_ROWS

        def rel_turns(engine, body, first, end):
            with engine.Fori(first, end) as turn:
                for s in range(REL_TURN):
                    body(turn * REL_TURN + s, turn, s)

        def load_edges(engine, to, array, here):
            full = (GROUPS - 1) * GROUP
            engine.dma_start(to[0:GROUPS - 1, :],
                             array[0:full].rearrange("(g e) -> g e", e=GROUP)).then_inc(here, 16)
            engine.dma_start(to[GROUPS - 1:GROUPS, 0:LAST_EDGES],
                             array[full:EDGES].rearrange("(g e) -> g e", g=1)).then_inc(here, 16)

        def y_bank(q):
            return (q + 4) % 8

        def msg_block(i):
            return row_space[:, columns(i, MSG_ALL)]

        def columns(i, width):
            return slice(i * width, (i + 1) * width) if isinstance(i, int) else bass.ds(i * width, width)

        def by_case(engine, windows_fit, every):
            case_value = engine.value_load(case_i[0:1, 0:1], min_val=0, max_val=1)
            with engine.If(case_value < 1):
                windows_fit()
            with engine.Else():
                every()

        def over_panels(engine, body):
            with engine.Fori(0, PANELS // 2 - 1) as turn:
                for parity in range(2):
                    body(turn * 2 + parity, turn, parity, PANEL)
            body(PANELS - 2, PANELS // 2 - 1, 0, PANEL)
            body(PANELS - 1, PANELS // 2 - 1, 1, LAST_PANEL)

        WORD_COLS = WORDS * TILES

        def load_words(sp, g, s, here):
            sp.dma_start(words[:, s, :, :].rearrange("p w t -> p (w t)"),
                         edge_table[:, columns(g, WORD_COLS)]).then_inc(here, 16)

        @block.sync
        def _(sp):
            def load_x(turn, half):
                first = turn * REL_TURN + half * 4
                sp.wait_ge(x_turned, first + 4)
                sp.dma_start(x_slots[:, half * 4:half * 4 + 4, :],
                             x[bass.ds(first * P, 4 * P), :].rearrange("(b p) f -> p b f", b=4))\
                  .then_inc(x_here[half], 16)

            def store_rows(i, turn, s):
                sp.wait_ge(rel_copied, i + 3)
                rows = LAST_ROWS if isinstance(i, int) and i == BLOCKS - 1 else P
                sp.dma_start(rel_table[bass.ds(i * P, rows), :], table_slots[0:rows, s % 4, :])\
                  .then_inc(rel_stored[s % 4], 16)
            load_x(0, 0)
            load_x(0, 1)
            sp.wait_ge(pads_set, 5)
            load_edges(sp, raw_dst_big.bitcast(I32), dst, dst_here)
            load_edges(sp, raw_dst.bitcast(I32), dst, dst_here)
            with sp.Fori(0, REL_TURNS - 1) as turn:
                for half in range(2):
                    for s in range(half * 4, half * 4 + 4):
                        if s % 4 == 2:
                            load_x(turn + 1, half)
                        store_rows(turn * REL_TURN + s, turn, s)
            for s in range(REL_TURN):
                if s == 4:
                    sp.wait_ge(x_turned, BLOCKS - 4)
                    sp.dma_start(x_slots[0:LAST_ROWS, 0, :], x[(BLOCKS - 1) * P:NODES, :])\
                      .then_inc(x_here[0], 16)
                store_rows((REL_TURNS - 1) * REL_TURN + s, REL_TURNS - 1, s)
            store_rows(BLOCKS - 1, REL_TURNS, 0)
            sp.wait_ge(words_stored, 16 * WORD_STORES)

            def words_layer0():
                with sp.Fori(0, ROUNDS) as r:
                    for s in range(SLOTS):
                        g = r * SLOTS + s
                        sp.wait_ge(one_window.added, g + 1)
                        load_words(sp, g, s, one_window.words_here[s])

            def words_all(layer):
                sems = all_windows[layer]

                def run():
                    with sp.Fori(0, GROUPS) as g:
                        sp.wait_ge(sems.added, g * WINDOWS + 1)
                        load_words(sp, g, 0, sems.words_here[0])
                return run

            by_case(sp, words_layer0, words_all(0))

            def counts_layer1():
                for s in range(2):
                    sp.wait_ge(counts_stored[s], 16 * (2 * ROUNDS + 1))

                def load_counts(k, turn, parity, groups):
                    for c in range(COUNT_CHUNKS):
                        sp.wait_ge(factors_ready, k * BLOCKS + (c + 1) * CHUNK_BLOCKS)
                        cols = slice(c * CHUNK_BLOCKS * WINDOW, (c + 1) * CHUNK_BLOCKS * WINDOW)
                        counts_from = count_table[bass.ds(k * PANEL, groups), :, cols]
                        sp.dma_start(counts[:, c, 0:groups, :], counts_from.rearrange("g p n -> p g n"))\
                          .then_inc(counts_here[c], 16)
                over_panels(sp, load_counts)

            def tables_layer1():
                sp.wait_ge(msg_biased, QUADS)

                def store_messages(i, r, s):
                    rows = LAST_ROWS if isinstance(i, int) and i == BLOCKS - 1 else P
                    sp.dma_start(msg_table[bass.ds(i * P, rows), :], msg_block(i)[0:rows, 0:MSG_ROW])\
                      .then_inc(msg_stored[s], 16)
                over_blocks(sp, store_messages)
                words_all(1)()
            by_case(sp, counts_layer1, tables_layer1)

            for q in range(QUADS):
                sp.wait_ge(out_dve, q + 1)
                sp.wait_ge(out_act, min(q + 1, QUADS - 1))
                to, partitions = quad_rows(out, q)
                sp.dma_start(to, node_rows[0:partitions, quad_cols(q)].rearrange("p (b f) -> p b f", f=FEAT))\
                  .then_inc(out_stored, 16)
            sp.wait_ge(out_stored, 16 * QUADS)

        @block.gpsimd
        def _(pool):
            pool.memset(ident[:, :], 0.0).then_inc(ident_made, 1)
            pool.memset(ones[:, :], 1.0).then_inc(consts_made, 1)
            pool.memset(eps[:, :], EPS).then_inc(consts_made, 1)
            pool.wait_ge(ident_made, 1)
            pool.affine_select(out=ident[:, :], in_=ident[:, :], compare_op=ALU.not_equal, fill=1.0,
                               base=0, pattern=[[-1, P]], channel_multiplier=1).then_inc(ident_made, 1)
            for t in range(TILES):
                last = pool.memset(tile_starts[:, t:t + 1], float(TILE_START[t]))
            last.then_inc(starts_made, 1)
            pool.memset(base_row[:, :], 0).then_inc(base_clear, 1)
            pool.wait_ge(pads_set, 5)
            load_edges(pool, raw_src.bitcast(I32), src, src_type_here)
            load_edges(pool, raw_type.bitcast(I32), edge_type, src_type_here)
            pool.dma_start(table_w[:, 0:FEAT], w_msg).then_inc(weights_here, 16)
            pool.dma_start(table_w[:, FEAT:MSG_ROW], w_att[0:FEAT, :]).then_inc(weights_here, 16)
            pool.dma_start(table_w[:, MSG_ROW:MSG_ALL], w_att[FEAT:2 * FEAT, :]).then_inc(weights_here, 16)
            pool.dma_start(att_dst[:, :], w_att[FEAT:2 * FEAT, :]).then_inc(weights_here, 16)
            pool.dma_start(table_bias[:, 0:FEAT],
                          b_msg.rearrange("(a f) -> a f", a=1).broadcast_to((P, b_msg.shape[0]))).then_inc(weights_here, 16)
            pool.dma_start(table_bias[:, FEAT:MSG_ROW],
                          b_att.rearrange("(a f) -> a f", a=1).broadcast_to((P, 1))).then_inc(weights_here, 16)
            pool.dma_start(w_ih_rows[:, :, :], w_ih.rearrange("(g p) f -> p g f", p=P)).then_inc(weights_here, 16)
            pool.dma_start(w_hh_rows[:, :, :], w_hh.rearrange("(g p) f -> p g f", p=P)).then_inc(weights_here, 16)
            pool.dma_start(b_ih_c[:, :], b_ih.rearrange("(g p) -> p g", p=P), allow_slow_non_contiguous=True).then_inc(weights_here, 16)
            pool.dma_start(b_hh_c[:, :], b_hh.rearrange("(g p) -> p g", p=P), allow_slow_non_contiguous=True).then_inc(weights_here, 16)
            pool.dma_start(gamma_c[:, :], gamma.rearrange("(p a) -> p a", a=1)).then_inc(weights_here, 16)
            pool.dma_start(beta_c[:, :], beta.rearrange("(p a) -> p a", a=1)).then_inc(weights_here, 16)
            pool.iota(window_iota_i[:, :], pattern=[[1, WINDOW]], base=0, channel_multiplier=0)\
                .then_inc(consts_made, 1)
            pool.iota(key_iota_i, pattern=[[1, KEYS]], base=0, channel_multiplier=0)\
                .then_inc(key_iota_made, 1)
            pool.iota(window_start_i[:, :], pattern=[[WINDOW, WINDOWS]], base=0, channel_multiplier=0)\
                .then_inc(consts_made, 1)
            pool.wait_ge(rel_copied, 8 + 2)
            load_edges(pool, raw_weight, edge_weight, edge_weights_here)
            pool.wait_ge(words_dve, TILES)
            pool.wait_ge(words_act, TILES)
            step = GROUPS // WORD_STORES
            for n in range(WORD_STORES):
                pool.wait_ge(rel_copied, (WORDS_TURN + n) * REL_TURN + 2)
                pool.dma_start(edge_table[:, columns(n, step * WORD_COLS)],
                               edge_words[:, columns(n, step), :, :].rearrange("p g w t -> p (g w t)"))\
                    .then_inc(words_stored, 16)
            pool.wait_ge(words_stored, 16 * WORD_STORES)
            pool.memset(sums_t[:, :], 0.0).then_inc(sums_clear, 1)

            def gather_group(table, width, plane, s, rows_here):
                pool.sem_inc(gathers_begun, 1)
                for t in range(TILES):
                    pool.indirect_dma_start(
                        out=gathered[:, s, t, 0:width], out_offset=None, in_=table,
                        in_offset=bass.IndirectOffsetOnAxis(ap=words[:, s, plane, t:t + 1].bitcast(U32),
                                                            axis=0)).then_inc(rows_here, 16)

            def gather_layer0():
                sems = one_window
                with pool.Fori(0, ROUNDS) as r:
                    for s in range(SLOTS):
                        pool.wait_ge(sems.words_here[s], (r + 1) * 16)
                        gather_group(rel_table_rows, FEAT, ROWS_WORD, s, sems.rows_here[s])

            def gather_all(layer, table, width):
                sems = all_windows[layer]

                def run():
                    with pool.Fori(0, GROUPS) as g:
                        pool.wait_ge(sems.words_here[0], (g + 1) * 16)
                        gather_group(table, width, ROWS_WORD + layer, 0, sems.rows_here[0])
                return run

            for s in range(4):
                pool.wait_ge(rel_stored[s], 16 * ((BLOCKS - 1) // 4 + (2 if s == 0 else 1)))
            pool.wait_ge(base_ready, 1)
            pool.wait_ge(consts_cast, 3)
            by_case(pool, gather_layer0, gather_all(0, rel_table_rows, FEAT))

            def clear_sums(q):
                pool.wait_ge(rows_added, q + 3)
                last_col = SUM_COLS if q == QUADS - 1 else quad_cols(q).stop
                pool.memset(sums_t[:, q * QUAD_COLS:last_col], 0.0).then_inc(sums_clear, 1)

            def bias_messages(q):
                blocks = quad_blocks(q)
                pool.wait_ge(msg_copied, blocks[-1] // 2 + 3)
                rows = row_space[:, blocks[0] * MSG_ALL:(blocks[-1] + 1) * MSG_ALL]\
                    .rearrange("p (b m) -> p b m", b=len(blocks))
                pool.tensor_add(rows, rows, table_bias[:, :].rearrange("p (b m) -> p b m", b=1)
                                .broadcast_to((P, len(blocks), MSG_ALL))).then_inc(msg_biased, 1)
            pool.wait_ge(weights_here, 12 * 16)
            for q in range(QUADS - 1 + AHEAD):
                if q < QUADS:
                    clear_sums(q)
                if q >= AHEAD:
                    bias_messages(q - AHEAD)

            def q_windows():
                def fill(k, turn, parity, groups):
                    pool.wait_ge(sigmoids_ready, (k + 1) * BLOCKS)
                    for i in range(groups):
                        base = pool.value_load(base_row[0:1, bass.ds(k * PANEL + PANEL + i, 1)], min_val=0,
                                               max_val=NODES - 1)
                        last = pool.tensor_copy(q_panel[:, parity, i * WINDOW:(i + 1) * WINDOW],
                                                att_rows[:, bass.ds(base, WINDOW)])
                    last.then_inc(q_ready, 1)
                pool.wait_ge(att_copied, QUADS + 2)
                pool.wait_ge(att_end_clear, 1)
                over_panels(pool, fill)

            def gather_messages():
                for s in range(4):
                    pool.wait_ge(msg_stored[s], 16 * ((BLOCKS - 1) // 4 + (2 if s == 0 else 1)))
                gather_all(1, msg_table, MSG_ROW)()
            by_case(pool, q_windows, gather_messages)

        @block.scalar
        def _(act):
            act.sem_inc(rel_copied, 2)
            act.sem_inc(xt_copied, 2)
            act.sem_inc(x1_copied, 2)
            act.sem_inc(counts_out, 1)
            act.sem_inc(sigmoids_ready, 2 * BLOCKS)
            for s in range(2):
                act.sem_inc(counts_stored[s], 16)
            for s in range(4):
                act.sem_inc(rel_stored[s], 16)
                act.sem_inc(msg_stored[s], 16)
            act.dma_start(rel_w[:, :, :], rel_emb.rearrange("r f o -> f r o")).then_inc(rel_w_here, 16)

            def copy_xt(i, turn, s):
                act.wait_ge(x_turned, i + 9)
                act.wait_ge(rel_mm, i + 1)
                nc.scalar.activation(xt_slots[:, s % 2, :], psum[:, 2 + s % 2, 0:P], ACT.Copy)\
                  .then_inc(xt_copied, 1)

            def evacuate(i, turn, s):
                act.wait_ge(rel_mm, i + 3)
                act.wait_ge(rel_stored[s % 4], (turn * 2 + s // 4 + 1) * 16)
                nc.scalar.activation(table_slots[:, s % 4, :].rearrange("p (h m) -> p h m", h=2),
                                     psum[:, 4 + 2 * (s % 2):6 + 2 * (s % 2), :], ACT.Copy)\
                  .then_inc(rel_copied, 1)

            def both(i, turn, s):
                copy_xt(i + 1, turn, (s + 1) % REL_TURN)
                evacuate(i, turn, s)
            copy_xt(0, 0, 0)
            rel_turns(act, both, 0, WORDS_TURN)
            for t in range(TILES):
                act.wait_ge(edges_turned, t + 1)
                nc.scalar.activation(
                    edge_words[:, :, ROWS_WORD:WORDS, t].rearrange("p g w -> p w g"),
                    psum[:, 2 + t % 2, 0:256].rearrange("p (w g) -> p w g", w=2)[:, :, 0:GROUPS],
                    ACT.Copy).then_inc(words_act, 1)
            rel_turns(act, both, WORDS_TURN, REL_TURNS)
            evacuate(BLOCKS - 1, REL_TURNS, 0)

            def counts_layer0():
                with act.Fori(0, ROUNDS) as r:
                    for s in range(SLOTS):
                        g = r * SLOTS + s
                        act.wait_ge(hot_used, g * TILES + TILES + HOT_SLOTS)
                        act.wait_ge(counts_stored[s % 2], (r * 2 + s // 2 + 1) * 16)
                        for c in range(BANKS):
                            last = nc.scalar.activation(
                                counts_out_slots[:, s % 2, c * BANK_COLS:c * BANK_COLS + bank_width(c)],
                                psum[:, 1 + c, 0:bank_width(c)], ACT.Copy)
                        last.then_inc(counts_out, 1)
                        act.wait_ge(counts_out, g + 2)
                        act.dma_start(count_table[bass.ds(g, 1), :, :].rearrange("a p n -> (a p) n"),
                                      counts_out_slots[:, s % 2, :]).then_inc(counts_stored[s % 2], 16)

            def nothing():
                act.nop()
            act.wait_ge(base_ready, 1)
            act.wait_ge(x_pads_clear, 1)
            act.wait_ge(gathers_begun, 1)
            act.wait_ge(words_dve, TILES)
            last_quad = (QUADS - 1) * QUAD_COLS
            act.dma_start(x_rows[:, 0:last_quad].rearrange("p (b f) -> p b f", f=FEAT),
                          x[0:last_quad, :].rearrange("(b p) f -> p b f", p=P)).then_inc(x_rows_here, 16)
            act.dma_start(x_rows[0:LAST_ROWS, last_quad:PADDED], x[last_quad:NODES, :]).then_inc(x_rows_here, 16)
            by_case(act, counts_layer0, nothing)
            act.drain().then_inc(sweep_done[0], 1)

            def deviations(n, batch):
                blocks = slice(batch[0] * QUAD, min(batch[1] * QUAD, BLOCKS))
                act.wait_ge(norm_step[n], 5)
                nc.scalar.activation(norm[:, 5, blocks], norm[:, 4, blocks], ACT.Sqrt, bias=eps[:, 0:1])\
                  .then_inc(std_ready[n], 1)

            def copy_att(q):
                act.wait_ge(att_mm, q + 1)
                nc.scalar.activation(att_rows[:, quad_cols(q)], psum[:, 6 + q % 2, 0:quad_width(q)], ACT.Copy)\
                  .then_inc(att_copied, 1)

            def copy_messages(q):
                for i in quad_blocks(q)[::2]:
                    act.wait_ge(msg_mm, i // 2 + 1)
                    cols = min(2, BLOCKS - i) * MSG_ALL
                    nc.scalar.activation(row_space[:, i * MSG_ALL:i * MSG_ALL + cols],
                                         psum[:, 4 + i // 2 % 2, 0:cols], ACT.Copy).then_inc(msg_copied, 1)
            for q in range(QUADS):
                for n, batch in enumerate(X1_BATCHES):
                    if batch[1] == q + AHEAD:
                        deviations(n, batch)
                act.wait_ge(x1_turned, q + 1)
                nc.scalar.activation(nodes_t[:, quad_cols(q)], psum[:, 2 + q % 2, 0:quad_width(q)], ACT.Copy)\
                  .then_inc(x1_copied, 1)
                if q >= 1:
                    copy_att(q - 1)
                    copy_messages(q - 1)
            copy_att(QUADS - 1)
            act.wait_ge(att_copied, QUADS + 2)
            act.wait_ge(att_end_clear, 1)

            def sigmoids_layer1():
                act.wait_ge(msg_biased, QUADS)

                def squash(k, turn, parity, groups):
                    act.wait_ge(q_ready, k + 1)
                    for b in range(BLOCKS):
                        act.wait_ge(factors_used, k * BLOCKS + b + 1)
                        nc.scalar.activation(factors[:, b % CHUNK_BLOCKS, 0:groups * WINDOW],
                                             q_panel[:, parity, 0:groups * WINDOW], ACT.Sigmoid,
                                             bias=msg_rows[:, b, FEAT:MSG_ROW]).then_inc(sigmoids_ready, 1)
                over_panels(act, squash)

            def sigmoids_all():
                sems = all_windows[1]
                with act.Fori(0, GROUPS) as g:
                    with act.Fori(0, WINDOWS) as w:
                        act.wait_ge(sems.rows_here[0], (g + 1) * (16 * TILES))
                        act.wait_ge(sems.added, g * WINDOWS + w + 1)
                        for t in range(TILES):
                            last = nc.scalar.activation(
                                select[:, 0, t, :], att_rows[:, bass.ds(w * WINDOW, WINDOW)],
                                ACT.Sigmoid, bias=gathered[:, 0, t, FEAT:MSG_ROW])
                        last.then_inc(sems.sigmoids_ready, 1)
            by_case(act, sigmoids_layer1, sigmoids_all)

            def gates(j, half):
                act.wait_ge(gates_mm, j + 1)
                act.wait_ge(h_ready, j + 1)
                for gate in range(2):
                    nc.scalar.activation(gru[:, half, gate, :], psum[:, 4 * half + gate, 0:CHUNK],
                                         ACT.Sigmoid, bias=gate_bias[:, gate:gate + 1]).then_inc(rz_ready, 1)
                act.wait_ge(n_input, j + 3)
                nc.scalar.activation(gru[:, half, 3, :], gru[:, half, 2, :], ACT.Tanh, bias=b_ih_c[:, 2:3])\
                  .then_inc(n_ready, 1)
            with act.Fori(0, CHUNKS // 2) as r:
                for half in (1, 0):
                    gates(r * 2 + 1 - half, half)

            act.wait_ge(bn_step, 1)
            nc.scalar.activation(bn[:, 2:3], bn[:, 1:2], ACT.Sqrt, bias=eps[:, 0:1]).then_inc(bn_std, 1)

            act.wait_ge(bn_ready, 1)

            def scale_h(q):
                nc.scalar.activation(sums_t[:, quad_cols(q)], sums_t[:, quad_cols(q)], ACT.Identity,
                                     bias=bn[:, 6:7], scale=bn[:, 4:5]).then_inc(y_scaled, 1)

            def out_rows(n):
                first, end = OUT_BATCHES[n]
                deviations(len(X1_BATCHES) + n, OUT_BATCHES[n])
                act.wait_ge(norm_step[len(X1_BATCHES) + n], 7)
                for q in range(first, end):
                    for i in quad_blocks(q)[1::2]:
                        last = nc.scalar.activation(node_rows[:, columns(i, P)], node_rows[:, columns(i, P)],
                                                    ACT.Identity, bias=norm[:, 1, i:i + 1],
                                                    scale=norm[:, 6, i:i + 1])
                    if len(quad_blocks(q)) > 1:
                        last.then_inc(out_act, 1)

            scale_h(0)
            scale_h(1)
            for q in range(QUADS):
                if q + 2 < QUADS:
                    scale_h(q + 2)
                act.wait_ge(y_turned, q + 1)
                nc.scalar.activation(node_rows[:, quad_cols(q)], psum[:, y_bank(q), 0:quad_width(q)], ACT.Copy)\
                  .then_inc(y_copied, 1)
                for n, (first, end) in enumerate(OUT_BATCHES):
                    if q == min(end + 1, QUADS - 1):
                        out_rows(n)

        @block.tensor
        def _(pe):
            pe.sem_inc(rel_mm, 2)
            pe.sem_inc(x_turned, REL_TURN)
            pe.sem_inc(one_window.summed, 2)
            pe.sem_inc(hot_used, HOT_SLOTS)
            pe.sem_inc(factors_used, CHUNK_BLOCKS)

            def turn_x(i, turn, s):
                pe.wait_ge(x_here[s // 4], (turn + 1) * 16)
                pe.wait_ge(xt_copied, i + 1)
                nc.tensor.transpose(psum[:, 2 + s % 2, 0:P], x_slots[:, s, :], ident[:, :])\
                  .then_inc(x_turned, 1)

            def multiply_x(i, turn, s):
                pe.wait_ge(xt_copied, i + 3)
                pe.wait_ge(rel_copied, i + 1)
                for half in range(2):
                    last = nc.tensor.matmul(psum[:, 4 + 2 * (s % 2) + half, :], xt_slots[:, s % 2, :],
                                            rel_w[:, 4 * half:4 * half + 4, :].rearrange("p r o -> p (r o)"),
                                            start=True, stop=True)
                last.then_inc(rel_mm, 1)

            def both(i, turn, s):
                turn_x(i + 1, turn + (s + 1) // REL_TURN, (s + 1) % REL_TURN)
                multiply_x(i, turn, s)
            pe.wait_ge(ident_made, 2)
            turn_x(0, 0, 0)
            pe.wait_ge(rel_w_here, 16)
            rel_turns(pe, both, 0, BASE_TURN)

            pe.wait_ge(consts_made, 4)
            pe.wait_ge(diag_ready, 2)
            for n in range(2):
                last = nc.tensor.matmul(psum[:, 0, n * GROUPS:(n + 1) * GROUPS], ones[0:GROUPS, :],
                                        diag[0:GROUPS, n, :], start=True, stop=True)
            last.then_inc(base_spread, 1)
            rel_turns(pe, both, BASE_TURN, WORDS_TURN)

            pe.wait_ge(planes_ready, 1)
            pe.wait_ge(edge_weights_here, 2 * 16)
            pe.wait_ge(xt_copied, WORDS_TURN * REL_TURN + 3)
            planes = (raw_dst, raw_weight, raw_key, raw_lo, raw_type, raw_src)
            for t in range(TILES):
                if t >= 2:
                    pe.wait_ge(words_act, t - 1)
                    pe.wait_ge(words_dve, t - 1)
                for w, plane in enumerate(planes):
                    last = nc.tensor.transpose(psum[:, t % 2 + 2 * (w // 4), (w % 4) * P:(w % 4) * P + GROUPS],
                                               plane[0:GROUPS, t * P:(t + 1) * P],
                                               ident[0:GROUPS, 0:GROUPS])
                last.then_inc(edges_turned, 1)

            pe.wait_ge(weights_here, 12 * 16)
            pe.wait_ge(words_dve, TILES)
            for gate in range(3):
                nc.tensor.transpose(psum[:, 0, gate * P:(gate + 1) * P], w_ih_rows[:, gate, :], ident[:, :])
                last = nc.tensor.transpose(psum[:, 1, gate * P:(gate + 1) * P], w_hh_rows[:, gate, :],
                                           ident[:, :])
            last.then_inc(gates_turned, 1)

            pe.wait_ge(words_act, TILES)
            rel_turns(pe, both, WORDS_TURN, REL_TURNS)
            multiply_x(BLOCKS - 1, REL_TURNS, 0)
            pe.wait_ge(gates_copied, 1)
            pe.wait_ge(base_ready, 1)
            pe.wait_ge(rel_copied, BLOCKS + 2)

            def sum_group(s, half, bank, sems):
                for t in range(TILES):
                    last = nc.tensor.matmul(psum[:, bank, 0:WINDOW], gathered[:, s, t, 0:FEAT],
                                            select[:, half, t, :], start=(t == 0), stop=(t == TILES - 1))
                last.then_inc(sems.summed, 1)

            def products_layer0():
                sems = one_window
                with pe.Fori(0, ROUNDS) as r:
                    for s in range(SLOTS):
                        g = r * SLOTS + s
                        pe.wait_ge(sems.rows_here[s], (r + 1) * (16 * TILES))
                        pe.wait_ge(sems.added, g + SLOTS)
                        pe.wait_ge(sems.select_ready, g + 3)
                        sum_group(s, s % 2, 0, sems)
                        pe.wait_ge(counts_out, g + 1)
                        for t in range(TILES):
                            pe.wait_ge(hot_ready, g * TILES + t + 1)
                            count_tile(t, (s * TILES + t) % HOT_SLOTS)

            def count_tile(t, slot):
                for c in range(BANKS):
                    blocks = min(BANK_BLOCKS, BLOCKS - c * BANK_BLOCKS)
                    to = psum[:, 1 + c, 0:BANK_COLS].rearrange("p (h w) -> p h w", h=BANK_BLOCKS)
                    keys = slice(c * BANK_BLOCKS * TILE_WINDOW, (c * BANK_BLOCKS + blocks) * TILE_WINDOW)
                    last = nc.tensor.matmul(
                        to[:, 0:blocks, TILE_START[t]:TILE_START[t] + TILE_WINDOW], lo_hot[:, slot, :],
                        key_hot[:, slot, keys].rearrange("p (h w) -> p h w", h=blocks),
                        start=(t == 0), stop=(t == TILES - 1), skip_group_check=True)
                last.then_inc(hot_used, 1)

            def products_layer1():
                pe.wait_ge(msg_biased, QUADS)

                def multiply(k, turn, parity, groups):
                    pe.wait_ge(panel_added, k * PANEL + 1)
                    for b in range(BLOCKS):
                        pe.wait_ge(factors_ready, (k + 1) * BLOCKS + b + 1)
                        nc.tensor.matmul(psum[:, parity, 0:groups * WINDOW], msg_rows[:, b, 0:FEAT],
                                         factors[:, b % CHUNK_BLOCKS, 0:groups * WINDOW],
                                         start=(b == 0), stop=(b == BLOCKS - 1)).then_inc(factors_used, 1)
                over_panels(pe, multiply)

            def sum_all(layer):
                sems = all_windows[layer]

                def run():
                    with pe.Fori(0, GROUPS) as g:
                        with pe.Fori(0, WINDOWS) as w:
                            pe.wait_ge(sems.rows_here[0], (g + 1) * (16 * TILES))
                            pe.wait_ge(sems.select_ready, g * WINDOWS + w + 1)
                            sum_group(0, 0, 0, sems)
                return run
            by_case(pe, products_layer0, sum_all(0))

            def turn_quad(q, bank, blocks_from):
                for n, i in enumerate(quad_blocks(q)):
                    last = nc.tensor.transpose(psum[:, bank, n * P:(n + 1) * P],
                                               blocks_from[:, columns(i, P)], ident[:, :])
                return last

            pe.wait_ge(sweep_done[0], 2)
            def turn_sums(q):
                pe.wait_ge(rows_added, q + 1)
                turn_quad(q, q % 2, sums_t).then_inc(sums_turned, 1)

            def multiply_x1(q):
                pe.wait_ge(x1_copied, q + 3)
                pe.wait_ge(att_copied, q + 1)
                nc.tensor.matmul(psum[:, 6 + q % 2, 0:quad_width(q)], att_dst_rep[:, :],
                                 nodes_t[:, quad_cols(q)], start=True, stop=True).then_inc(att_mm, 1)
                for i in quad_blocks(q):
                    pair = i // 2
                    if i % 2 == 0:
                        pe.wait_ge(msg_copied, pair + 1)
                    last = nc.tensor.matmul(
                        psum[:, 4 + pair % 2, i % 2 * MSG_ALL:(i % 2 + 1) * MSG_ALL],
                        nodes_t[:, columns(i, P)], table_w[:, :], start=True, stop=True)
                    if i % 2 == 1 or i == BLOCKS - 1:
                        last.then_inc(msg_mm, 1)

            pe.wait_ge(rep_ready, 1)
            for q in range(AHEAD):
                turn_sums(q)
            for q in range(QUADS):
                if q + AHEAD < QUADS:
                    turn_sums(q + AHEAD)
                pe.wait_ge(x1_rows_ready, q + 1)
                pe.wait_ge(x1_copied, q + 1)
                turn_quad(q, 2 + q % 2, node_rows).then_inc(x1_turned, 1)
                if q >= 1:
                    multiply_x1(q - 1)
            multiply_x1(QUADS - 1)

            by_case(pe, products_layer1, sum_all(1))

            def gate_products(j, half, first):
                pe.wait_ge(n_input, j + 1)
                cols = bass.ds(j * CHUNK, CHUNK)
                for gate in range(3):
                    nc.tensor.matmul(psum[:, 4 * half + gate, 0:CHUNK], w_hh_t[:, gate, :], nodes_t[:, cols],
                                     start=True, stop=(gate == 2))
                if first:
                    pe.wait_ge(sweep_done[1], 1)
                for gate in range(2):
                    nc.tensor.matmul(psum[:, 4 * half + gate, 0:CHUNK], w_ih_t[:, gate, :], sums_t[:, cols],
                                     start=False, stop=True)
                nc.tensor.matmul(psum[:, 4 * half + 3, 0:CHUNK], w_ih_t[:, 2, :], sums_t[:, cols],
                                 start=True, stop=True).then_inc(gates_mm, 1)
            gate_products(0, 1, True)
            gate_products(1, 0, False)
            with pe.Fori(1, CHUNKS // 2) as r:
                for half in (1, 0):
                    gate_products(r * 2 + 1 - half, half, False)

            def y_part(q, blocks_from, first):
                for n, i in enumerate(quad_blocks(q)):
                    last = nc.tensor.matmul(psum[:, y_bank(q), n * P:(n + 1) * P], blocks_from[:, columns(i, P)],
                                            ident[:, :], start=(first and n == 0), stop=not first,
                                            skip_group_check=True)
                return last
            for q in range(8):
                if q % 4 == 0:
                    pe.wait_ge(n_input, CHUNKS + 1 + q // 4)
                y_part(q, nodes_t, True)
            for q in range(QUADS):
                pe.wait_ge(y_scaled, q + 1)
                y_part(q, sums_t, False).then_inc(y_turned, 1)
                if 8 <= q + 6 < QUADS:
                    pe.wait_ge(y_copied, q - 1)
                    y_part(q + 6, nodes_t, True)

        @block.vector
        def _(dve):
            v = nc.vector
            dve.sem_inc(rows_added, 2)
            dve.sem_inc(msg_copied, 2)
            dve.sem_inc(att_copied, 2)
            dve.sem_inc(h_ready, 2)
            dve.sem_inc(n_input, 2)
            dve.sem_inc(one_window.select_ready, 2)
            dve.sem_inc(one_window.added, SLOTS)
            dve.sem_inc(factors_ready, BLOCKS)
            dve.sem_inc(panel_added, 1)
            for layer in range(2):
                dve.sem_inc(all_windows[layer].added, 1)

            tail = slice(LAST_EDGES, GROUP)
            v.memset(x_rows[:, (QUADS - 1) * QUAD_COLS:PADDED], 0.0).then_inc(x_pads_clear, 1)
            v.memset(table_bias[:, MSG_ROW:MSG_ALL], 0.0).then_inc(bias_clear, 1)
            v.memset(raw_dst_big.bitcast(I32)[96:P, tail], 1 << 20).then_inc(pads_set, 1)
            v.memset(raw_dst.bitcast(I32)[96:P, tail], int(NO_MATCH)).then_inc(pads_set, 1)
            v.memset(raw_src[96:P, tail], 0.0).then_inc(pads_set, 1)
            v.memset(raw_type[96:P, tail], 0.0).then_inc(pads_set, 1)
            v.memset(raw_weight[96:P, tail], 0.0).then_inc(pads_set, 1)
            g = slice(0, GROUPS)
            steps = [0]

            def step(*instructions):
                for instruction in instructions:
                    instruction.then_inc(prep_step, 1)
                steps[0] += len(instructions)
                dve.wait_ge(prep_step, steps[0])

            def tiles(raw):
                return raw[g, :].rearrange("g (t e) -> g t e", t=TILES)
            starts = tile_starts[g, :]
            dve.wait_ge(dst_here, 4 * 16)
            dve.wait_ge(starts_made, 1)
            step(v.tensor_reduce(lo[g, 0:TILES], tiles(raw_dst_big.bitcast(I32)), AX.X, ALU.min),
                 v.tensor_reduce(hi[g, :], tiles(raw_dst.bitcast(I32)), AX.X, ALU.max))
            step(v.tensor_reduce(lo[g, TILES:TILES + 1], lo[g, 0:TILES], AX.X, ALU.min),
                 v.tensor_sub(hi[g, :], hi[g, :], starts),
                 v.tensor_sub(low_miss[g, :], starts, lo[g, 0:TILES]))
            group_lo = lo[g, TILES:TILES + 1]
            step(v.tensor_scalar(hi[g, :], hi[g, :], group_lo, float(TILE_WINDOW - 1), ALU.subtract, ALU.subtract),
                 v.tensor_scalar(low_miss[g, :], low_miss[g, :], group_lo, None, ALU.add))
            step(v.tensor_tensor(miss[g, 0:TILES], hi[g, :], low_miss[g, :], ALU.max))
            step(v.tensor_reduce(miss[g, TILES:TILES + 1], miss[g, 0:TILES], AX.X, ALU.max))
            dve.wait_ge(ident_made, 2)
            v.tensor_scalar(diag[g, 0, :], ident[g, g], group_lo, None, ALU.mult).then_inc(diag_ready, 1)
            v.tensor_scalar(diag[g, 1, :], ident[g, g], miss[g, TILES:TILES + 1], None, ALU.mult)\
             .then_inc(diag_ready, 1)

            dve.wait_ge(src_type_here, 4 * 16)
            step(v.tensor_scalar(raw_lo.bitcast(I32)[g, :], raw_src.bitcast(I32)[g, :], P - 1, None,
                                 ALU.bitwise_and),
                 v.tensor_scalar(raw_key.bitcast(I32)[g, :], raw_src.bitcast(I32)[g, :], 7, None,
                                 ALU.arith_shift_right))
            step(v.tensor_copy(raw_lo[g, :], raw_lo.bitcast(I32)[g, :]),
                 v.tensor_copy(raw_src[g, :], raw_src.bitcast(I32)[g, :]),
                 v.tensor_copy(raw_dst[g, :], raw_dst.bitcast(I32)[g, :]))
            step(v.scalar_tensor_tensor(raw_type[g, :], raw_src[g, :], float(RELS), raw_type.bitcast(I32)[g, :],
                                        ALU.mult, ALU.add))
            dve.wait_ge(base_spread, 1)
            step(v.tensor_reduce(case[:, 0:1], psum[:, 0, GROUPS:2 * GROUPS], AX.X, ALU.max))
            step(v.tensor_scalar(case[:, 1:2], case[:, 0:1], 0.0, None, ALU.is_le),
                 v.tensor_scalar(case[:, 0:1], case[:, 0:1], 0.0, None, ALU.is_gt))
            dve.wait_ge(base_clear, 1)
            step(v.tensor_mul(group_base[g, :], group_lo, case[g, 1:2]),
                 v.tensor_copy(case_i[:, :], case[:, 0:1]),
                 v.tensor_scalar(base_row[:, PANEL:PANEL + GROUPS], psum[:, 0, 0:GROUPS], case[:, 1:2], None, ALU.mult))
            step(v.tensor_scalar(raw_dst[g, :], raw_dst[g, :], group_base[g, :], None, ALU.subtract))
            step(v.scalar_tensor_tensor(raw_key[g, :], raw_key.bitcast(I32)[g, :], float(TILE_WINDOW),
                                        raw_dst[g, :], ALU.mult, ALU.add))
            v.tensor_sub(tiles(raw_key), tiles(raw_key),
                         starts.rearrange("g (t e) -> g t e", e=1).broadcast_to((GROUPS, TILES, P)))\
             .then_inc(planes_ready, 1)
            dve.drain().then_inc(base_ready, 1)

            for t in range(TILES):
                dve.wait_ge(edges_turned, t + 1)
                v.tensor_copy(edge_words[:, :, 0:ROWS_WORD, t].rearrange("p g w -> p w g").bitcast(F32),
                              psum[:, t % 2, :].rearrange("p (w g) -> p w g", w=ROWS_WORD)[:, :, 0:GROUPS])\
                 .then_inc(words_dve, 1)

            dve.wait_ge(consts_made, 4)
            v.tensor_copy(window_iota[:, :], window_iota_i[:, :]).then_inc(consts_cast, 1)
            v.tensor_copy(window_start[:, :], window_start_i[:, :]).then_inc(consts_cast, 1)

            dve.wait_ge(key_iota_made, 1)
            v.tensor_copy(key_iota, key_iota_i).then_inc(consts_cast, 1)

            dve.wait_ge(gates_turned, 1)
            v.tensor_copy(w_ih_t[:, :, :].rearrange("p g o -> p (g o)"), psum[:, 0, 0:3 * P])
            v.tensor_copy(w_hh_t[:, :, :].rearrange("p g o -> p (g o)"), psum[:, 1, 0:3 * P])
            v.tensor_add(gate_bias[:, :], b_ih_c[:, 0:2], b_hh_c[:, 0:2])
            v.tensor_scalar(att_dst_rep[:, :], ones[:, :], att_dst[:, 0:1], None, ALU.mult)\
             .then_inc(rep_ready, 1)
            dve.drain().then_inc(gates_copied, 1)

            def select_tile(layer, t, s, half, places):
                if layer == 0:
                    return v.tensor_scalar(select[:, half, t, :], window_iota[:, :], places[:, t:t + 1],
                                           words_f[:, s, 1, t:t + 1], ALU.is_equal, ALU.mult)
                return v.scalar_tensor_tensor(select[:, half, t, :], window_iota[:, :], places[:, t:t + 1],
                                              select[:, half, t, :], ALU.is_equal, ALU.mult)

            def add_window(entry, columns_from, added, done):
                base = dve.value_load(base_row[0:1, bass.ds(entry, 1)], min_val=0, max_val=NODES - 1)
                dve.wait_ge(added, done)
                to = sums_t[:, bass.ds(base, WINDOW)]
                v.tensor_add(to, to, columns_from).then_inc(added, 1)

            def layer0():
                sems = one_window

                def select_group(g, r, s):
                    dve.wait_ge(sems.words_here[s], (r + 1) * 16)
                    dve.wait_ge(sems.summed, g + 1)
                    for t in range(TILES):
                        last = select_tile(0, t, s, s % 2, words_f[:, s, 0, :])
                    last.then_inc(sems.select_ready, 1)

                def group(g, r, s, select_next):
                    if select_next:
                        select_group(g + 1, r + (s + 1) // SLOTS, (s + 1) % SLOTS)
                    for t in range(TILES):
                        slot = (s * TILES + t) % HOT_SLOTS
                        dve.wait_ge(hot_used, g * TILES + t + 1)
                        v.tensor_scalar(key_hot[:, slot, :], key_iota, words_f[:, s, 2, t:t + 1],
                                        None, ALU.is_equal)
                        v.tensor_scalar(lo_hot[:, slot, :], key_iota[:, 0:P],
                                        words_f[:, s, 3, t:t + 1], None, ALU.is_equal).then_inc(hot_ready, 1)
                    dve.wait_ge(sems.summed, g + 3)
                    add_window(g + PANEL, psum[:, 0, 0:WINDOW], sems.added, g + SLOTS)

                select_group(0, 0, 0)
                with dve.Fori(0, ROUNDS - 1) as r:
                    for s in range(SLOTS):
                        group(r * SLOTS + s, r, s, True)
                for s in range(SLOTS):
                    group((ROUNDS - 1) * SLOTS + s, ROUNDS - 1, s, s < SLOTS - 1)

            def layer1():
                v.memset(psum[:, 1, 0:PANEL_COLS], 0.0).then_inc(bank_clear, 1)
                dve.wait_ge(bank_clear, 1)

                def scale(k, turn, parity, groups):
                    for b in range(BLOCKS):
                        c = b // CHUNK_BLOCKS
                        factor = factors[:, b % CHUNK_BLOCKS, 0:groups * WINDOW]\
                            .rearrange("p (g w) -> p g w", g=groups)
                        cols = slice(b % CHUNK_BLOCKS * WINDOW, (b % CHUNK_BLOCKS + 1) * WINDOW)
                        if b % CHUNK_BLOCKS == 0:
                            dve.wait_ge(counts_here[c], (k + 1) * 16)
                        dve.wait_ge(sigmoids_ready, (k + 2) * BLOCKS + b + 1)
                        v.tensor_mul(factor, factor, counts[:, c, 0:groups, cols]).then_inc(factors_ready, 1)
                        if b in range(3, 3 + 2 * PANEL, 2):
                            add_before(k, (b - 3) // 2, 1 - parity)

                def add_before(k, i, bank):
                    if i == 0:
                        dve.wait_ge(factors_used, k * BLOCKS + CHUNK_BLOCKS)
                    add_window(k * PANEL + i, psum[:, bank, i * WINDOW:(i + 1) * WINDOW], panel_added,
                               k * PANEL + i + 1)
                over_panels(dve, scale)
                for i in range(LAST_PANEL):
                    add_before(PANELS, i, 1)

            def sweep_all(layer):
                sems = all_windows[layer]

                def run():
                    with dve.Fori(0, GROUPS) as g:
                        with dve.Fori(0, WINDOWS) as w:
                            dve.wait_ge(sems.words_here[0], (g + 1) * 16)
                            done = g * WINDOWS + w
                            dve.wait_ge(sems.added, done + 1)
                            v.tensor_scalar(in_window[:, :], words_f[:, 0, 0, :],
                                            window_start[:, bass.ds(w, 1)], None, ALU.subtract)\
                             .then_inc(sems.shifted, 1)
                            dve.wait_ge(sems.shifted, done + 1)
                            if layer == 1:
                                dve.wait_ge(sems.sigmoids_ready, done + 1)
                            for t in range(TILES):
                                last = select_tile(layer, t, 0, 0, in_window)
                            last.then_inc(sems.select_ready, 1)
                            dve.wait_ge(sems.summed, done + 1)
                            to = sums_t[:, bass.ds(w * WINDOW, WINDOW)]
                            v.tensor_add(to, to, psum[:, 0, 0:WINDOW]).then_inc(sems.added, 1)
                return run

            dve.wait_ge(consts_cast, 3)
            dve.wait_ge(sums_clear, 1)
            by_case(dve, layer0, sweep_all(0))
            dve.drain().then_inc(sweep_done[0], 1)

            def quad_stats(q, done):
                for i in quad_blocks(q):
                    last = v.bn_stats(stats[:, i, :], node_rows[:, columns(i, P)])
                last.then_inc(done, 1)

            def add_rows(q):
                dve.wait_ge(sums_turned, q + 1)
                v.tensor_add(node_rows[:, quad_cols(q)], x_rows[:, quad_cols(q)],
                             psum[:, q % 2, 0:quad_width(q)]).then_inc(rows_added, 1)
                dve.wait_ge(rows_added, q + 3)
                quad_stats(q, row_stats)

            def normalisers(n, first, end, quads_done):
                sems = norm_step[n]
                b = slice(first * QUAD, min(end * QUAD, BLOCKS))
                dve.wait_ge(quads_done, end)
                v.tensor_add(norm[:, 1, b], stats[:, b, 1], stats[:, b, 4]).then_inc(sems, 1)
                v.tensor_sub(norm[:, 2, b], stats[:, b, 1], stats[:, b, 4]).then_inc(sems, 1)
                v.tensor_add(norm[:, 3, b], stats[:, b, 2], stats[:, b, 5]).then_inc(sems, 1)
                dve.wait_ge(sems, 3)
                v.tensor_scalar(norm[:, 0, b], norm[:, 1, b], 0.5, None, ALU.mult)
                v.tensor_scalar(norm[:, 3, b], norm[:, 3, b], 1.0 / FEAT, None, ALU.mult)
                v.scalar_tensor_tensor(norm[:, 7, b], norm[:, 2, b], 0.25, norm[:, 2, b], ALU.mult, ALU.mult)\
                 .then_inc(sems, 1)
                dve.wait_ge(sems, 4)
                v.tensor_add(norm[:, 4, b], norm[:, 7, b], norm[:, 3, b]).then_inc(sems, 1)
                dve.wait_ge(std_ready[n], 1)
                v.reciprocal(norm[:, 6, b], norm[:, 5, b]).then_inc(sems, 1)
                dve.wait_ge(sems, 6)
                v.scalar_tensor_tensor(norm[:, 1, b], norm[:, 0, b], -1.0, norm[:, 6, b], ALU.mult, ALU.mult)\
                 .then_inc(sems, 1)

            def x1_rows(q):
                for i in quad_blocks(q):
                    last = v.tensor_scalar(node_rows[:, columns(i, P)], node_rows[:, columns(i, P)],
                                           norm[:, 0, i:i + 1], norm[:, 6, i:i + 1],
                                           ALU.subtract, ALU.mult)
                last.then_inc(x1_rows_ready, 1)

            dve.wait_ge(x_rows_here, 32)
            for q in range(QUADS):
                add_rows(q)
                for n, (first, end) in enumerate(X1_BATCHES):
                    if q == end - 1:
                        normalisers(n, first, end, row_stats)
                        for b in range(first, end):
                            x1_rows(b)
            dve.wait_ge(msg_mm, (BLOCKS - 1) // 2 + 1)
            v.tensor_add(msg_block(BLOCKS - 1), psum[:, 4 + (BLOCKS - 1) // 2 % 2, 0:MSG_ALL], table_bias[:, :])\
             .then_inc(msg_biased, 1)
            v.memset(att_rows[:, PADDED:SUM_COLS], 0.0).then_inc(att_end_clear, 1)

            dve.wait_ge(sums_clear, 1 + QUADS)
            by_case(dve, layer1, sweep_all(1))
            dve.drain().then_inc(sweep_done[1], 1)

            def input_gate(j, half):
                slot = gru[:, half, :, :]
                dve.wait_ge(rz_ready, j * 2 + 2)
                v.scalar_tensor_tensor(slot[:, 4, :], psum[:, 4 * half + 2, 0:CHUNK], b_hh_c[:, 2:3],
                                       slot[:, 0, :], ALU.add, ALU.mult).then_inc(n_step, 1)
                dve.wait_ge(n_step, j + 1)
                v.tensor_add(slot[:, 2, :], slot[:, 4, :], psum[:, 4 * half + 3, 0:CHUNK]).then_inc(n_input, 1)

            def update(j, half, valid):
                cols = bass.ds(j * CHUNK, CHUNK)
                slot = gru[:, half, :, :]
                dve.wait_ge(n_ready, j + 1)
                v.tensor_sub(slot[:, 5, :], nodes_t[:, cols], slot[:, 3, :]).then_inc(h_step, 1)
                dve.wait_ge(h_step, j * 2 + 1)
                v.tensor_mul(slot[:, 5, :], slot[:, 5, :], slot[:, 1, :]).then_inc(h_step, 1)
                dve.wait_ge(h_step, j * 2 + 2)
                v.tensor_add(sums_t[:, cols], slot[:, 5, :], slot[:, 3, :]).then_inc(h_ready, 1)
                dve.wait_ge(h_ready, j + 3)
                v.bn_stats(bn_stats[:, columns(j, 1), :].rearrange("p i s -> p (i s)"),
                           sums_t[:, bass.ds(j * CHUNK, valid)]).then_inc(h_stats, 1)
            input_gate(0, 1)
            with dve.Fori(0, CHUNKS // 2 - 1) as r:
                for half in (1, 0):
                    input_gate(r * 2 + 2 - half, 1 - half)
                    update(r * 2 + 1 - half, half, CHUNK)
            input_gate(CHUNKS - 1, 0)
            update(CHUNKS - 2, 1, CHUNK)
            update(CHUNKS - 1, 0, NODES - (CHUNKS - 1) * CHUNK)

            dve.wait_ge(h_stats, CHUNKS)
            v.bn_aggr(bn[:, 0:2], bn_stats[:, :, :].rearrange("p j s -> p (j s)")).then_inc(bn_step, 1)
            dve.wait_ge(bn_std, 1)
            v.reciprocal(bn[:, 3:4], bn[:, 2:3]).then_inc(bn_step, 1)
            dve.wait_ge(bn_step, 2)
            v.tensor_mul(bn[:, 4:5], bn[:, 3:4], gamma_c[:, :]).then_inc(bn_step, 1)
            dve.wait_ge(bn_step, 3)
            v.tensor_mul(bn[:, 5:6], bn[:, 0:1], bn[:, 4:5]).then_inc(bn_step, 1)
            dve.wait_ge(bn_step, 4)
            v.tensor_sub(bn[:, 6:7], beta_c[:, :], bn[:, 5:6]).then_inc(bn_ready, 1)

            for n, (first, end) in enumerate(OUT_BATCHES):
                for q in range(first, end):
                    dve.wait_ge(y_copied, q + 1)
                    quad_stats(q, y_stats)
                normalisers(len(X1_BATCHES) + n, first, end, y_stats)
                dve.wait_ge(norm_step[len(X1_BATCHES) + n], 7)
                for q in range(first, end):
                    for i in quad_blocks(q)[::2]:
                        last = v.tensor_scalar(node_rows[:, columns(i, P)], node_rows[:, columns(i, P)],
                                               norm[:, 0, i:i + 1], norm[:, 6, i:i + 1],
                                               ALU.subtract, ALU.mult)
                    last.then_inc(out_dve, 1)


INPUTS = ["x", "src", "dst", "edge_type_8", "edge_weight", "L0_gnn_rel_emb", "L1_gnn_W_msg",
          "L1_gnn_b_msg", "L1_gnn_W_att", "L1_gnn_b_att", "L1_gnn_W_ih", "L1_gnn_b_ih",
          "L1_gnn_W_hh", "L1_gnn_b_hh", "L1_gnn_gamma", "L1_gnn_beta"]


def kernel(**inputs):
    import numpy as np
    import concourse.bacc as bacc
    from concourse import mybir as mb
    from concourse.bass_utils import run_bass_kernel_spmd

    nc = bacc.Bacc("TRN2", target_bir_lowering=False, num_devices=1)
    arrays, args = {}, []
    for name in INPUTS:
        a = np.ascontiguousarray(inputs[name])
        arrays[f"in_{name}"] = a
        args.append(nc.dram_tensor(f"in_{name}", a.shape, mb.dt.from_np(a.dtype), kind="ExternalInput").ap())
    out = nc.dram_tensor("out", (NODES, FEAT), F32, kind="ExternalOutput").ap()
    build(nc, *args, out)
    result = run_bass_kernel_spmd(nc, [arrays], core_ids=[0])
    return result.results[0]["out"]
```
